# Optimizing a Trainium2 kernel written in Bass

```python
import numpy as np
import jax
import jax.numpy as jnp

def _softmax(x, axis=-1):
    return jax.nn.softmax(x, axis=axis)

def _gelu(x):
    return jax.nn.gelu(x, approximate=True)

def _silu(x):
    return jax.nn.silu(x)

def _sigmoid(x):
    return jax.nn.sigmoid(x)

def _layernorm(x, axis=-1, eps=1e-05):
    m = jnp.mean(x, axis=axis, keepdims=True)
    v = jnp.var(x, axis=axis, keepdims=True)
    return (x - m) / jnp.sqrt(v + eps)

def _scatter_add(tgt, idx, src, axis=0):
    return tgt.at[idx].add(src)

def _segment_sum(src, seg, n):
    return jax.ops.segment_sum(src, seg, n)
kernel_name = 'mk_prb_d1_jaxref_r4_5b9f2b'

def setup_inputs(seed: int=0):
    np.random.seed(seed)
    _w = jnp.asarray

    def _L0_attn_setup():
        import jax, jax.numpy as jnp
        import numpy as np
        HIDDEN = 256
        HEADS = 16
        HEAD_DIM = HIDDEN // HEADS
        SCALE = HEAD_DIM ** (-0.5)
        key = jax.random.key(seed)
        ks = jax.random.split(key, 9)
        init = 1.0 / np.sqrt(HIDDEN)
        hidden_states = jax.random.normal(ks[0], (8, 256, HIDDEN), dtype=jnp.float32)

        def lin(k):
            kw, kb = jax.random.split(k)
            W = jax.random.uniform(kw, (HIDDEN, HIDDEN), jnp.float32, -init, init)
            b = jax.random.uniform(kb, (HIDDEN,), jnp.float32, -init, init)
            return (W, b)
        Wq, bq = lin(ks[1])
        Wk, bk = lin(ks[2])
        Wv, bv = lin(ks[3])
        Wo, bo = lin(ks[4])
        return {'hidden_states': hidden_states, 'Wq': Wq, 'bq': bq, 'Wk': Wk, 'bk': bk, 'Wv': Wv, 'bv': bv, 'Wo': Wo, 'bo': bo}
    _L0_attn_in = _L0_attn_setup()

    def _L0_ffn_setup():
        import jax, jax.numpy as jnp
        import numpy as np
        import math
        GOLDEN_CENTER = 1.0 / math.e
        GOLDEN_LOWER = 0.5 - math.log(4.0 / 3.0)
        GOLDEN_UPPER = 0.5
        B, T, D = (4, 512, 256)
        E = 8
        I = 1024 // (E // 2)

        def _routing_weights(x, Wr, temperature):
            inh = jax.nn.sigmoid(x @ Wr / temperature)
            in_zone = (inh >= GOLDEN_LOWER) & (inh <= GOLDEN_UPPER)
            dist = jnp.abs(inh - GOLDEN_CENTER)
            w = jnp.exp(-dist / 0.1) * in_zone.astype(x.dtype)
            wsum = w.sum(axis=-1, keepdims=True)
            no_expert = wsum < 1e-08
            fb = jnp.exp(-dist / 0.3)
            _, top2 = jax.lax.top_k(fb, 2)
            fb_mask = jax.nn.one_hot(top2, E, dtype=x.dtype).sum(axis=-2)
            fb_w = fb * fb_mask
            fb_w = fb_w / jnp.clip(fb_w.sum(axis=-1, keepdims=True), 1e-08)
            w = jnp.where(no_expert, fb_w, w)
            wsum = w.sum(axis=-1, keepdims=True)
            return w / jnp.clip(wsum, 1e-08)
        key = jax.random.key(seed)
        k = jax.random.split(key, 6)
        s_d = 1.0 / math.sqrt(D)
        s_i = 1.0 / math.sqrt(I)
        return {'x': jax.random.normal(k[0], (B, T, D), jnp.float32), 'Wg': jax.random.normal(k[1], (E, D, I), jnp.float32) * s_d, 'Wu': jax.random.normal(k[2], (E, D, I), jnp.float32) * s_d, 'Wd': jax.random.normal(k[3], (E, I, D), jnp.float32) * s_i, 'Wr': jax.random.normal(k[4], (D, E), jnp.float32) * s_d, 'temperature': jnp.ones((1,), jnp.float32)}
    _L0_ffn_in = _L0_ffn_setup()
    _d = {'L0_attn_hidden_states': _L0_attn_in['hidden_states'], 'L0_attn_Wq': _L0_attn_in['Wq'], 'L0_attn_bq': _L0_attn_in['bq'], 'L0_attn_Wk': _L0_attn_in['Wk'], 'L0_attn_bk': _L0_attn_in['bk'], 'L0_attn_Wv': _L0_attn_in['Wv'], 'L0_attn_bv': _L0_attn_in['bv'], 'L0_attn_Wo': _L0_attn_in['Wo'], 'L0_attn_bo': _L0_attn_in['bo'], 'L0_ffn_Wg': _L0_ffn_in['Wg'], 'L0_ffn_Wu': _L0_ffn_in['Wu'], 'L0_ffn_Wd': _L0_ffn_in['Wd'], 'L0_ffn_Wr': _L0_ffn_in['Wr'], 'L0_ffn_temperature': _L0_ffn_in['temperature']}
    _x0 = _d['L0_attn_hidden_states']
    _d['L0_attn_hidden_states'] = jax.random.normal(jax.random.fold_in(jax.random.key(seed), 1), (2, 4096, 256), dtype=_x0.dtype)
    del _x0
    return _d

def reference(L0_attn_hidden_states, L0_attn_Wq, L0_attn_bq, L0_attn_Wk, L0_attn_bk, L0_attn_Wv, L0_attn_bv, L0_attn_Wo, L0_attn_bo, L0_ffn_Wg, L0_ffn_Wu, L0_ffn_Wd, L0_ffn_Wr, L0_ffn_temperature):

    def _L0_attn_ref(hidden_states, Wq, bq, Wk, bk, Wv, bv, Wo, bo):
        import jax, jax.numpy as jnp
        import numpy as np
        HIDDEN = 256
        HEADS = 16
        HEAD_DIM = HIDDEN // HEADS
        SCALE = HEAD_DIM ** (-0.5)
        b, s, d = hidden_states.shape
        q = (hidden_states @ Wq.T + bq).reshape(b, s, HEADS, HEAD_DIM)
        k = (hidden_states @ Wk.T + bk).reshape(b, s, HEADS, HEAD_DIM)
        v = (hidden_states @ Wv.T + bv).reshape(b, s, HEADS, HEAD_DIM)
        q = q * SCALE
        scores = jnp.einsum('bqhd,bkhd->bhqk', q, k)
        probs = jax.nn.softmax(scores.astype(jnp.float32), axis=-1).astype(scores.dtype)
        out = jnp.einsum('bhqk,bkhd->bqhd', probs, v).reshape(b, s, d)
        return out @ Wo.T + bo

    def _L0_ffn_ref(x, Wg, Wu, Wd, Wr, temperature):
        import jax, jax.numpy as jnp
        import numpy as np
        import math
        GOLDEN_CENTER = 1.0 / math.e
        GOLDEN_LOWER = 0.5 - math.log(4.0 / 3.0)
        GOLDEN_UPPER = 0.5
        B, T, D = (4, 512, 256)
        E = 8
        I = 1024 // (E // 2)

        def _routing_weights(x, Wr, temperature):
            inh = jax.nn.sigmoid(x @ Wr / temperature)
            in_zone = (inh >= GOLDEN_LOWER) & (inh <= GOLDEN_UPPER)
            dist = jnp.abs(inh - GOLDEN_CENTER)
            w = jnp.exp(-dist / 0.1) * in_zone.astype(x.dtype)
            wsum = w.sum(axis=-1, keepdims=True)
            no_expert = wsum < 1e-08
            fb = jnp.exp(-dist / 0.3)
            _, top2 = jax.lax.top_k(fb, 2)
            fb_mask = jax.nn.one_hot(top2, E, dtype=x.dtype).sum(axis=-2)
            fb_w = fb * fb_mask
            fb_w = fb_w / jnp.clip(fb_w.sum(axis=-1, keepdims=True), 1e-08)
            w = jnp.where(no_expert, fb_w, w)
            wsum = w.sum(axis=-1, keepdims=True)
            return w / jnp.clip(wsum, 1e-08)
        weights = _routing_weights(x, Wr, temperature)
        gate = jnp.einsum('btd,edi->beti', x, Wg)
        up = jnp.einsum('btd,edi->beti', x, Wu)
        h = jax.nn.silu(gate) * up
        e_out = jnp.einsum('beti,eid->betd', h, Wd)
        out = jnp.einsum('bte,betd->btd', weights, e_out)
        return out
    x = L0_attn_hidden_states
    xn = _layernorm(x, axis=-1)
    x = x + _L0_attn_ref(xn, L0_attn_Wq, L0_attn_bq, L0_attn_Wk, L0_attn_bk, L0_attn_Wv, L0_attn_bv, L0_attn_Wo, L0_attn_bo) + _L0_ffn_ref(xn, L0_ffn_Wg, L0_ffn_Wu, L0_ffn_Wd, L0_ffn_Wr, L0_ffn_temperature)
    return x

_drawn_inputs = setup_inputs


def setup_inputs(seed=0):
    import zlib

    import numpy as np

    out = dict(_drawn_inputs(seed))
    spreads = {}
    factors = {'L0_attn_Wq': 8.0,
     'L0_attn_bq': 8.0,
     'L0_attn_Wk': 8.0,
     'L0_attn_bk': 64.0,
     'L0_attn_Wv': 6.714,
     'L0_attn_bv': 2.761,
     'L0_attn_bo': 3.59}
    for name, (base, spread) in spreads.items():
        noise = np.random.default_rng([zlib.crc32(name.encode()), seed]).standard_normal(out[name].shape)
        drawn = base * np.exp(spread * noise) if base else spread * noise
        out[name] = jnp.asarray(drawn.astype(out[name].dtype))
    for name, factor in factors.items():
        out[name] = (out[name] * factor).astype(out[name].dtype)
    return out
```

```python
import concourse.bass as bass
from concourse import mybir
from contextlib import ExitStack

F32 = mybir.dt.float32
BF16 = mybir.dt.bfloat16
F32R = mybir.dt.float32r
ALU = mybir.AluOpType
ACT = mybir.ActivationFunctionType
AX = mybir.AxisListType

P = 128
B, S, D = 2, 4096, 256
H, HD = 16, 16
E, FI = 8, 256
TOK = B * S
KC = D // P
GT = 512
NG = TOK // GT
TPG = GT // P
NT = TOK // P
HEADS = B * H
QB = S // GT
KB = S // P
QUAD = 4
QUADS = KB // QUAD
MAXW = 1024
MAXU = S // MAXW
UNITS = TPG * MAXU
PAIRS = ((0, 0), (0, 1), (1, 0), (1, 1), (0, 2), (2, 0))
ROWS = len(PAIRS) * HD
ROWSM = ROWS + 2
VC = 32
PRING = 2 * QUAD
SCALE = HD ** -0.5
EPS = 1e-5
CENTER, LOWER, UPPER = 0.36787944117144233, 0.5 - 0.28768207245178085, 0.5
TINY = 1e-8
DMA = 16


def tools(nc, ctx):
    def sb(name, shape, dt):
        return ctx.enter_context(nc.sbuf_tensor(name, shape, dt))

    def pb(name, shape, dt):
        return ctx.enter_context(nc.psum_tensor(name, shape, dt))

    def sem(name):
        return ctx.enter_context(nc.semaphore(name))

    return sb, pb, sem


def wait_alone(engine, sem, value, passed):
    engine.wait_ge(sem, value)
    engine.sem_inc(passed, 1)


def product(nc, out, lhs, rhs, low_low=False):
    terms = [(a, b) for k in range(len(lhs)) for a, b in ((0, 0), (0, 1), (1, 0)) + (((1, 1),) if low_low else ())]
    terms = [(k, a, b) for k in range(len(lhs)) for a, b in terms[:len(terms) // len(lhs)]]
    for n, (k, a, b) in enumerate(terms):
        last = nc.tensor.matmul(out, lhs[k][a], rhs[k][b], start=(n == 0), stop=(n == len(terms) - 1))
    return last


def setup_phase(nc, a, c):
    with ExitStack() as ctx:
        sb, pb, sem = tools(nc, ctx)
        wnat = sb("wnat", [P, 4, KC, D], F32)
        raw = [sb(f"raw{n}", [P, E, KC, FI], F32) for n in range(3)]
        wr = sb("wr", [P, KC, E], F32)
        bq, temp = sb("bq", [P, KC], F32), sb("temp", [P, 1], F32)
        psT = [pb(f"psT{i}", [P, 512], F32) for i in range(2)]
        s_w = sem("w_loaded")
        s_raw = [sem(f"experts_loaded{n}") for n in range(3)]
        s_zero = sem("zeroed")
        s_id = sem("identity_ready")
        s_const = sem("constants_ready")
        s_t = sem("weight_transposed")
        s_high = sem("high_ready")
        s_low = sem("low_ready")
        s_ehigh = sem("expert_high_ready")
        s_small = sem("small_loaded")
        block = ctx.enter_context(nc.Block())
        experts = ("Wg", "Wu", "Wd")

        def load_experts(engine, n):
            engine.dma_start(raw[n][:, :, :, :], a[experts[n]].rearrange("e (c p) i -> p e c i", p=P)).then_inc(s_raw[n], DMA)

        @block.sync
        def _(sp):
            for n, name in enumerate(("Wq", "Wk", "Wv", "Wo")):
                sp.dma_start(wnat[:, n, :, :], a[name].rearrange("(c p) i -> p c i", p=P)).then_inc(s_w, DMA)
            sp.dma_start(bq[:, :], a["bq"].rearrange("(c p) -> p c", p=P), allow_slow_non_contiguous=True).then_inc(s_small, DMA)
            sp.dma_start(c.bk[:, :], a["bk"].rearrange("(c p) -> p c", p=P), allow_slow_non_contiguous=True).then_inc(s_small, DMA)
            sp.dma_start(c.bv[:, :], a["bv"].partition_broadcast(P)).then_inc(s_small, DMA)
            sp.dma_start(c.bo[:, :], a["bo"].partition_broadcast(P)).then_inc(s_small, DMA)
            sp.dma_start(temp[:, :], a["temperature"].partition_broadcast(P)).then_inc(s_small, DMA)
            sp.dma_start(wr[:, :, :], a["Wr"].rearrange("(c p) e -> p c e", p=P)).then_inc(s_small, DMA)

        @block.gpsimd
        def _(pool):
            nc.gpsimd.memset(c.ident[:, :], 0.0).then_inc(s_zero, 1)
            nc.gpsimd.memset(c.before[:, :, :], 1.0).then_inc(s_zero, 1)
            pool.wait_ge(s_zero, 2)
            nc.gpsimd.affine_select(out=c.ident[:, :], in_=c.ident[:, :], compare_op=ALU.not_equal, fill=1.0,
                                    base=0, pattern=[[-1, P]], channel_multiplier=1).then_inc(s_id, 1)
            nc.gpsimd.affine_select(out=c.before[:, :, :], in_=c.before[:, :, :], compare_op=ALU.is_gt, fill=0.0,
                                    base=0, pattern=[[1, E], [-1, E]], channel_multiplier=0).then_inc(s_id, 1)
            pool.wait_ge(s_ehigh, 3 * 2)
            nc.gpsimd.tensor_tensor(c.experts[1][:, 2, E - 2:, :, :], raw[2][:, E - 2:, :, :], c.experts[0][:, 2, E - 2:, :, :], ALU.subtract).then_inc(s_id, 1)

        @block.tensor
        def _(pe):
            pe.wait_ge(s_id, 1)
            pe.wait_ge(s_w, 4 * DMA)
            for n in range(4):
                for i in range(KC):
                    u = KC * n + i
                    if u >= 2:
                        pe.wait_ge(s_low, u - 1)
                    for o in range(KC):
                        last = nc.tensor.transpose(psT[u % 2][:, o * P:(o + 1) * P], wnat[:, n, o, i * P:(i + 1) * P], c.ident[:, :])
                    last.then_inc(s_t, 1)

        @block.scalar
        def _(act):
            for n in range(3):
                load_experts(act, n)
            for u in range(3 * KC):
                act.wait_ge(s_t, u + 1)
                nc.scalar.activation(c.wT[u // KC][0][:, u % KC, :], psT[u % 2][:, 0:D], ACT.Identity).then_inc(s_high, 1)
            for n in range(3):
                act.wait_ge(s_raw[n], DMA)
                for e0 in (0, E // 2):
                    nc.scalar.activation(c.experts[0][:, n, e0:e0 + E // 2, :, :], raw[n][:, e0:e0 + E // 2, :, :], ACT.Identity).then_inc(s_ehigh, 1)

        @block.vector
        def _(dve):
            for n in range(3):
                for i in range(KC):
                    u = KC * n + i
                    dve.wait_ge(s_high, u + 1)
                    nc.vector.tensor_tensor(c.wT[n][1][:, i, :], psT[u % 2][:, 0:D], c.wT[n][0][:, i, :], ALU.subtract).then_inc(s_low, 1)
            for i in range(KC):
                u = KC * 3 + i
                dve.wait_ge(s_t, u + 1)
                nc.vector.tensor_copy(c.woT[:, i, :], psT[u % 2][:, 0:D]).then_inc(s_low, 1)
            dve.wait_ge(s_id, 1)
            nc.vector.tensor_copy(c.identb[:, :], c.ident[:, :]).then_inc(s_const, 1)
            nc.vector.memset(c.eps[:, :], EPS).then_inc(s_const, 1)
            dve.wait_ge(s_small, 6 * DMA)
            nc.vector.tensor_scalar(c.bqs[:, :], bq[:, :], SCALE, None, ALU.mult).then_inc(s_const, 1)
            nc.vector.reciprocal(c.rtemp[:, :], temp[:, :]).then_inc(s_const, 1)
            nc.vector.tensor_copy(c.wr[0][:, :, :], wr[:, :, :]).then_inc(s_const, 1)
            dve.wait_ge(s_const, 5)
            nc.vector.tensor_tensor(c.wr[1][:, :, :], wr[:, :, :], c.wr[0][:, :, :], ALU.subtract).then_inc(s_const, 1)
            for n in range(3):
                for half, e0 in enumerate((0, E // 2)):
                    e1 = E - 2 if n == 2 and e0 else e0 + E // 2
                    dve.wait_ge(s_ehigh, 2 * n + half + 1)
                    nc.vector.tensor_tensor(c.experts[1][:, n, e0:e1, :, :], raw[n][:, e0:e1, :, :], c.experts[0][:, n, e0:e1, :, :],
                                            ALU.subtract).then_inc(s_const, 1)


MISC = (("x", 0, "dve"), ("x", 1, "dve"), ("route", 0, "dve"), ("q", 0, "act"), ("q", 1, "act"),
        ("k", 0, "act"), ("k", 1, "act"), ("v", 0, "dve"), ("v", 1, "dve"))
MISC_AFTER = {1: (0, 1), 2: (2,), 3: (3, 4), 5: (5, 6), 7: (7, 8)}
MISC_ACT = sum(m[2] == "act" for m in MISC)
MISC_DVE = len(MISC) - MISC_ACT
SPLITS = 2 * KC
LINKS = 25


def emptied(n):
    return sum(m[2] == MISC[n][2] for m in MISC[:n + 1])


def token_phase(nc, a, c):
    with ExitStack() as ctx:
        sb, pb, sem = tools(nc, ctx)
        x_in = [sb(f"x_in{i}", [P, TPG, D], F32) for i in range(2)]
        base = [sb(f"base{i}", [P, TPG, D], F32) for i in range(2)]
        xn = sb("xn", [P, TPG, D], F32)
        xT = [[sb(f"xT{i}{hl}", [P, KC, GT], F32R) for hl in range(2)] for i in range(2)]
        full = [sb(f"full{i}", [P, GT], F32) for i in range(2)]
        rest = [sb(f"rest{i}", [P, GT], F32) for i in range(2)]
        part = [sb(f"part{i}", [P, 3, GT], BF16) for i in range(2)]
        gated = [sb(f"gated{i}", [P, GT], F32) for i in range(2)]
        hraw = [sb(f"hraw{i}", [P, GT], F32) for i in range(2)]
        hid = [[sb(f"hid{i}{hl}", [P, KC, GT], F32R) for hl in range(2)] for i in range(2)]
        v_sb = [sb(f"v_sb{i}", [P, 2, D], F32) for i in range(2)]
        stats = sb("stats", [P, TPG, 6], F32)
        mv = sb("mv", [P, TPG, 2], F32)
        std = sb("std", [P, TPG], F32)
        rstd = sb("rstd", [P, TPG], F32)
        rt = sb("rt", [P, 10, TPG, E], F32)
        rs = sb("rs", [P, 6, TPG], F32)
        beats = sb("beats", [P, 2, TPG, E, E], F32)
        wts = [sb(f"wts{i}", [P, TPG, E], F32) for i in range(2)]
        misc = [pb(f"misc{i}", [P, 512], F32) for i in range(2)]
        gate = [pb(f"gate{i}", [P, GT], F32) for i in range(2)]
        up = [pb(f"up{i}", [P, GT], F32) for i in range(2)]
        down = [pb(f"down{i}", [P, 2, D], F32) for i in range(2)]

        x_loaded = [sem(f"x_loaded{i}") for i in range(2)]
        stats_done = sem("stats_done")
        std_done = sem("std_done")
        xn_done = sem("xn_done")
        xh_ready = sem("xT_high_ready")
        misc_full = sem("misc_full")
        misc_act = sem("misc_act")
        misc_dve = sem("misc_dve")
        dist_ready = sem("dist_ready")
        exp_given = sem("exp_given")
        rest_ready = sem("rest_ready")
        second_ready = sem("second_ready")
        parts_ready = sem("parts_ready")
        parts_stored = [sem(f"parts_stored{i}") for i in range(2)]
        gu_full = sem("gate_up_full")
        silu_done = sem("silu_done")
        hid_ready = sem("hid_ready")
        hh_ready = sem("hid_high_ready")
        hl_ready = sem("hid_low_ready")
        v_stored = [sem(f"v_stored{i}") for i in range(2)]
        down_full = sem("down_full")
        down_used = sem("down_used")
        base_init = sem("base_init")
        base_stored = [sem(f"base_stored{i}") for i in range(2)]
        vchain = sem("vector_chain")
        passed = sem("passed")

        block = ctx.enter_context(nc.Block())

        def rolled(engine, before, body):
            before()
            with engine.Fori(0, NG // 2 - 1) as gg:
                body(2 * gg, 0, False, True)
                body(2 * gg + 1, 1, False, True)
            body(NG - 2, 0, False, False)
            body(NG - 1, 1, True, False)

        def tokens_of(dram, g):
            return dram[bass.ds(g * GT, GT), :].rearrange("(t p) d -> p t d", p=P)

        @block.sync
        def _(sp):
            def load(g, par):
                sp.dma_start(x_in[par][:, :, :], tokens_of(a["x"], g)).then_inc(x_loaded[par], DMA)

            def store_parts(g):
                for u in range(SPLITS):
                    w, half = divmod(u, KC)
                    wait_alone(sp, parts_ready, g * SPLITS + u + 1 + 2, passed)
                    sp.dma_start(c.parts_d[w, :, half * P:(half + 1) * P, bass.ds(g * GT, GT)].rearrange("r p t -> p r t"),
                                 part[u % 2][:, :, :]).then_inc(parts_stored[u % 2], DMA)

            def store_v(g):
                for i in range(2):
                    wait_alone(sp, misc_dve, g * MISC_DVE + emptied(len(MISC) - 2 + i), passed)
                    sp.dma_start(c.v_d[bass.ds(g * GT + 2 * i * P, 2 * P), :].rearrange("(t p) d -> p t d", p=P),
                                 v_sb[i][:, :, :]).then_inc(v_stored[i], DMA)

            def before():
                for i in range(2):
                    sp.sem_inc(base_stored[i], DMA)
                    sp.sem_inc(parts_stored[i], DMA)
                    sp.sem_inc(v_stored[i], DMA)
                load(0, 0)
                load(1, 1)
                store_parts(0)
                store_v(0)

            def body(g, par, last, more):
                if more:
                    sp.wait_ge(xn_done, g + 1)
                    wait_alone(sp, base_init, g + 1, passed)
                    load(g + 2, par)
                if not last:
                    store_parts(g + 1)
                    store_v(g + 1)
                wait_alone(sp, down_used, (g + 1) * E * 2 + 2, passed)
                sp.dma_start(tokens_of(c.base_d, g), base[par][:, :, :]).then_inc(base_stored[par], DMA)

            rolled(sp, before, body)
            for i in range(2):
                sp.wait_ge(base_stored[i], (NG // 2 + 1) * DMA)
                sp.wait_ge(parts_stored[i], (SPLITS // 2 * NG + 1) * DMA)
                sp.wait_ge(v_stored[i], (NG + 1) * DMA)

        def pieces(pair, c0=0, cols=None):
            return [[v[:, k, c0:c0 + cols if cols else None] for v in pair] for k in range(KC)]

        def tile_of(pair, t):
            return pieces(pair, t * P, P)

        @block.tensor
        def _(pe):
            def misc_unit(g, par, n, first):
                kind, i, _ = MISC[n]
                if n >= 2:
                    prev = n - 2
                    pe.wait_ge(misc_act if MISC[prev][2] == "act" else misc_dve,
                               g * (MISC_ACT if MISC[prev][2] == "act" else MISC_DVE) + emptied(prev))
                elif not first:
                    pe.wait_ge(misc_dve, (g - 1) * MISC_DVE + emptied(len(MISC) - 2 + n))
                bank = misc[(par * len(MISC) + n) % 2]
                if kind == "x":
                    pe.wait_ge(xn_done, g + 1)
                    for t in range(TPG):
                        last = nc.tensor.transpose(bank[:, t * P:(t + 1) * P], xn[:, t, i * P:(i + 1) * P], c.ident[:, :])
                elif kind == "route":
                    pe.wait_ge(misc_dve, g * MISC_DVE + KC)
                    for t in range(TPG):
                        last = product(nc, bank[:, t * E:(t + 1) * E], tile_of(xT[par], t), pieces(c.wr), low_low=True)
                elif kind in "qk":
                    last = product(nc, bank[:, :], pieces(c.wT["qk".index(kind)], i * P, P), pieces(xT[par]))
                else:
                    for j in range(2):
                        last = product(nc, bank[:, j * D:(j + 1) * D], tile_of(xT[par], 2 * i + j), pieces(c.wT[2]))
                last.then_inc(misc_full, 1)

            def expert(w, e, c0, cols):
                return [[v[:, w, e, k, c0:c0 + cols] for v in c.experts] for k in range(KC)]

            def gate_up(g, par, e):
                for half in range(KC):
                    pe.wait_ge(hid_ready, (g * E + e) * KC + half + 1)
                    for w, bank in ((0, gate[half]), (1, up[half])):
                        last = product(nc, bank[:, :], expert(w, e, half * P, P), pieces(xT[par]))
                    last.then_inc(gu_full, 1)

            def down_proj(g, e):
                idx = g * E + e
                pe.wait_ge(hl_ready, idx * KC + KC + 2)
                for hf in range(2):
                    pe.wait_ge(down_used, idx * 2 + hf + 1)
                    for j in range(2):
                        t = 2 * hf + j
                        last = product(nc, down[hf][:, j, :], tile_of(hid[e % 2], t), expert(2, e, 0, D))
                    last.then_inc(down_full, 1)

            def before():
                for n in range(len(MISC)):
                    misc_unit(0, 0, n, True)

            def body(g, par, last, more):
                for e in range(E):
                    gate_up(g, par, e)
                    if e:
                        down_proj(g, e - 1)
                    if not last:
                        for n in MISC_AFTER.get(e, ()):
                            misc_unit(g + 1, 1 - par, n, False)
                down_proj(g, E - 1)

            rolled(pe, before, body)

        @block.scalar
        def _(act):
            def root(g):
                act.wait_ge(stats_done, g + 1)
                nc.scalar.activation(std[:, :], mv[:, :, 1], ACT.Sqrt, bias=c.eps[:, 0:1]).then_inc(std_done, 1)

            def misc_unit(g, par, n):
                kind, i, _ = MISC[n]
                if kind == "route":
                    act.wait_ge(misc_dve, g * MISC_DVE + emptied(n))
                    nc.scalar.activation(rt[:, 1, :, :], rt[:, 0, :, :], ACT.Exp, scale=-1.0).then_inc(exp_given, 1)
                    act.wait_ge(dist_ready, g + 1)
                    nc.scalar.activation(rt[:, 6, :, :], rt[:, 5, :, :], ACT.Exp, scale=-1.0 / 0.1).then_inc(exp_given, 1)
                    nc.scalar.activation(rt[:, 7, :, :], rt[:, 5, :, :], ACT.Exp, scale=-1.0 / 0.3).then_inc(exp_given, 1)
                    return
                if kind == "v":
                    return
                act.wait_ge(misc_full, g * len(MISC) + n + 1)
                bank = misc[(par * len(MISC) + n) % 2]
                if kind == "x":
                    nc.scalar.activation(xT[par][0][:, i, :], bank[:, :], ACT.Identity).then_inc(xh_ready, 1)
                    return
                u = (0 if kind == "q" else KC) + i
                bias, scale = (c.bqs, SCALE) if kind == "q" else (c.bk, 1.0)
                act.wait_ge(rest_ready, g * SPLITS + u + 1)
                nc.scalar.activation(full[u % 2][:, :], bank[:, :], ACT.Identity, bias=bias[:, i:i + 1], scale=scale)
                act.wait_ge(parts_stored[u % 2], (g * (SPLITS // 2) + u // 2 + 1) * DMA)
                nc.scalar.activation(part[u % 2][:, 0, :], bank[:, :], ACT.Identity, bias=bias[:, i:i + 1],
                                     scale=scale).then_inc(misc_act, 1)

            def before():
                root(0)
                for n in range(len(MISC)):
                    misc_unit(0, 0, n)

            def body(g, par, last, more):
                for e in range(E):
                    for half in range(KC):
                        act.wait_ge(gu_full, (g * E + e) * KC + half + 1)
                        nc.scalar.activation(gated[half][:, :], gate[half][:, :], ACT.Silu).then_inc(silu_done, 1)
                    for half in range(KC):
                        act.wait_ge(hid_ready, (g * E + e) * KC + half + 1 + 2)
                        nc.scalar.activation(hid[e % 2][0][:, half, :], hraw[half][:, :], ACT.Identity).then_inc(hh_ready, 1)
                    if not last:
                        if e == 0:
                            root(g + 1)
                        for n in MISC_AFTER.get(e, ()):
                            misc_unit(g + 1, 1 - par, n)

            rolled(act, before, body)

        @block.gpsimd
        def _(pool):
            def base_start(g, par):
                pool.wait_ge(x_loaded[par], (g // 2 + 1) * DMA)
                pool.wait_ge(base_stored[par], (g // 2 + 1) * DMA)
                for t in range(TPG):
                    ins = nc.gpsimd.tensor_tensor(base[par][:, t, :], x_in[par][:, t, :], c.bo[:, :], ALU.add)
                ins.then_inc(base_init, 1)

            def misc_unit(g, n):
                kind, i, _ = MISC[n]
                if kind in ("q", "k"):
                    u = (0 if kind == "q" else KC) + i
                    wait_alone(pool, rest_ready, g * SPLITS + u + 1 + 2, passed)
                    nc.gpsimd.tensor_copy(part[u % 2][:, 1, :], rest[u % 2][:, :]).then_inc(second_ready, 1)
                    pool.wait_ge(second_ready, g * SPLITS + u + 1)
                    nc.gpsimd.tensor_tensor(part[u % 2][:, 2, :], rest[u % 2][:, :], part[u % 2][:, 1, :],
                                            ALU.subtract).then_inc(parts_ready, 1)

            def before():
                pool.sem_inc(parts_ready, 2)
                pool.sem_inc(hl_ready, 2)
                base_start(0, 0)
                for n in range(len(MISC)):
                    misc_unit(0, n)

            def body(g, par, last, more):
                for e in range(E):
                    for half in range(KC):
                        pool.wait_ge(hh_ready, (g * E + e) * KC + half + 1)
                        nc.gpsimd.tensor_tensor(hid[e % 2][1][:, half, :], hraw[half][:, :], hid[e % 2][0][:, half, :],
                                                ALU.subtract).then_inc(hl_ready, 1)
                    if not last:
                        if e == 0:
                            base_start(g + 1, 1 - par)
                        for n in MISC_AFTER.get(e, ()):
                            misc_unit(g + 1, n)

            rolled(pool, before, body)

        @block.vector
        def _(dve):
            def step(instruction, s, value):
                instruction.then_inc(s, 1)
                dve.wait_ge(s, value)

            def norm(g, par, first):
                dve.wait_ge(x_loaded[par], (g // 2 + 1) * DMA)
                for t in range(TPG):
                    ins = nc.vector.bn_stats(stats[:, t, :], x_in[par][:, t, :])
                ins.then_inc(vchain, 1)
                wait_alone(dve, vchain, g * LINKS + 1, passed)
                for t in range(TPG):
                    ins = nc.vector.bn_aggr(mv[:, t, :], stats[:, t, :])
                ins.then_inc(stats_done, 1)
                dve.wait_ge(std_done, g + 1)
                step(nc.vector.reciprocal(rstd[:, :], std[:, :]), vchain, g * LINKS + 2)
                if not first:
                    dve.wait_ge(misc_dve, (g - 1) * MISC_DVE + KC)
                for t in range(TPG):
                    ins = nc.vector.tensor_scalar(xn[:, t, :], x_in[par][:, t, :], mv[:, t, 0:1], rstd[:, t:t + 1],
                                                  ALU.subtract, ALU.mult)
                ins.then_inc(xn_done, 1)

            def route(g, par, n):
                count = [2]

                def link(instruction):
                    count[0] += 1
                    step(instruction, vchain, g * LINKS + count[0])

                z, ez, den, inh, off, dist, w, fb, zone, rank = (rt[:, i, :, :] for i in range(10))
                wsum, none, some, fsum, total, rtotal = (rs[:, i, :] for i in range(6))

                def over(v):
                    return v.unsqueeze(2).broadcast_to([P, TPG, E])

                dve.wait_ge(misc_full, g * len(MISC) + n + 1)
                bank = misc[(par * len(MISC) + n) % 2]
                nc.vector.tensor_scalar(z, bank[:, 0:TPG * E].rearrange("p (t e) -> p t e", e=E), c.rtemp[:, 0:1], None,
                                        ALU.mult).then_inc(misc_dve, 1)
                dve.wait_ge(exp_given, g * 3 + 1)
                link(nc.vector.tensor_scalar(den, ez, 1.0, None, ALU.add))
                link(nc.vector.reciprocal(inh, den))
                link(nc.vector.tensor_scalar(off, inh, CENTER, None, ALU.subtract))
                nc.vector.scalar_tensor_tensor(out=dist, in0=off, scalar=-1.0, in1=off, op0=ALU.mult, op1=ALU.max).then_inc(dist_ready, 1)
                link(nc.vector.tensor_scalar(zone, inh, UPPER, None, ALU.is_le))
                link(nc.vector.scalar_tensor_tensor(out=zone, in0=inh, scalar=LOWER, in1=zone, op0=ALU.is_ge, op1=ALU.mult))
                dve.wait_ge(exp_given, g * 3 + 3)
                link(nc.vector.tensor_tensor(w, w, zone, ALU.mult))
                link(nc.vector.tensor_reduce(wsum, w, AX.X, ALU.add))
                link(nc.vector.tensor_scalar(none, wsum, TINY, None, ALU.is_lt))
                nc.vector.tensor_scalar(some, none, -1.0, 1.0, ALU.mult, ALU.add)
                for t in range(TPG):
                    mine = fb[:, t, :].unsqueeze(2).broadcast_to([P, E, E])
                    other = fb[:, t, :].unsqueeze(1).broadcast_to([P, E, E])
                    nc.vector.tensor_tensor(beats[:, 0, t, :, :], other, mine, ALU.is_gt)
                    ins = nc.vector.tensor_tensor(beats[:, 1, t, :, :], other, mine, ALU.is_ge)
                link(ins)
                for t in range(TPG):
                    ins = nc.vector.tensor_tensor(beats[:, 1, t, :, :], beats[:, 1, t, :, :], c.before[:, :, :], ALU.mult)
                link(ins)
                link(nc.vector.tensor_tensor(beats[:, 0, :, :, :], beats[:, 0, :, :, :], beats[:, 1, :, :, :], ALU.max))
                link(nc.vector.tensor_reduce(rank, beats[:, 0, :, :, :], AX.X, ALU.add))
                link(nc.vector.scalar_tensor_tensor(out=fb, in0=rank, scalar=2.0, in1=fb, op0=ALU.is_lt, op1=ALU.mult))
                link(nc.vector.tensor_reduce(fsum, fb, AX.X, ALU.add))
                link(nc.vector.tensor_scalar(fsum, fsum, TINY, None, ALU.max))
                link(nc.vector.reciprocal(total, fsum))
                link(nc.vector.tensor_tensor(total, total, none, ALU.mult))
                nc.vector.tensor_tensor(w, w, over(some), ALU.mult)
                link(nc.vector.tensor_tensor(fb, fb, over(total), ALU.mult))
                link(nc.vector.tensor_tensor(w, w, fb, ALU.add))
                link(nc.vector.tensor_reduce(wsum, w, AX.X, ALU.add))
                link(nc.vector.tensor_scalar(rtotal, wsum, TINY, None, ALU.max))
                return w, rtotal, over, link, count

            def misc_unit(g, par, n):
                kind, i, _ = MISC[n]
                if kind == "x":
                    dve.wait_ge(xh_ready, g * KC + i + 1)
                    nc.vector.tensor_tensor(xT[par][1][:, i, :], misc[(par * len(MISC) + n) % 2][:, :], xT[par][0][:, i, :],
                                            ALU.subtract).then_inc(misc_dve, 1)
                elif kind == "route":
                    w, rtotal, over, link, count = route(g, par, n)
                    link(nc.vector.reciprocal(rs[:, 0, :], rtotal))
                    link(nc.vector.tensor_tensor(wts[par][:, :, :], w, over(rs[:, 0, :]), ALU.mult))
                    assert count[0] == LINKS, count
                elif kind in ("q", "k"):
                    u = (0 if kind == "q" else KC) + i
                    dve.wait_ge(misc_act, g * MISC_ACT + emptied(n))
                    dve.wait_ge(parts_ready, g * SPLITS + u + 1)
                    nc.vector.tensor_tensor(rest[u % 2][:, :], full[u % 2][:, :], part[u % 2][:, 0, :],
                                            ALU.subtract).then_inc(rest_ready, 1)
                elif kind == "v":
                    dve.wait_ge(misc_full, g * len(MISC) + n + 1)
                    bank = misc[(par * len(MISC) + n) % 2]
                    dve.wait_ge(v_stored[i], (g + 1) * DMA)
                    nc.vector.tensor_tensor(v_sb[i][:, :, :], bank[:, :].rearrange("p (t d) -> p t d", d=D),
                                            c.bv[:, :].unsqueeze(1).broadcast_to([P, 2, D]), ALU.add).then_inc(misc_dve, 1)

            def add_expert(g, par, e):
                idx = g * E + e
                dve.wait_ge(down_used, idx * 2 + 2)
                if e == 0:
                    dve.wait_ge(base_init, g + 1)
                for hf in range(2):
                    dve.wait_ge(down_full, idx * 2 + hf + 1)
                    for j in range(2):
                        t = 2 * hf + j
                        ins = nc.vector.scalar_tensor_tensor(out=base[par][:, t, :], in0=down[hf][:, j, :], scalar=wts[par][:, t, e:e + 1],
                                                             in1=base[par][:, t, :], op0=ALU.mult, op1=ALU.add)
                    ins.then_inc(down_used, 1)

            def before():
                dve.sem_inc(rest_ready, 2)
                dve.sem_inc(hid_ready, 2)
                dve.sem_inc(down_used, 2)
                norm(0, 0, True)
                for n in range(len(MISC)):
                    misc_unit(0, 0, n)

            def body(g, par, last, more):
                for e in range(E):
                    for half in range(KC):
                        dve.wait_ge(silu_done, (g * E + e) * KC + half + 1)
                        dve.wait_ge(hl_ready, (g * E + e) * KC + half + 1)
                        nc.vector.tensor_tensor(hraw[half][:, :], gated[half][:, :], up[half][:, :], ALU.mult).then_inc(hid_ready, 1)
                    if e:
                        add_expert(g, par, e - 1)
                    if not last:
                        if e == 0:
                            norm(g + 1, 1 - par, False)
                        for n in MISC_AFTER.get(e, ()):
                            misc_unit(g + 1, 1 - par, n)
                add_expert(g, par, E - 1)

            rolled(dve, before, body)


def attention_phase(nc, a, c):
    with ExitStack() as ctx:
        sb, pb, sem = tools(nc, ctx)
        RING = 3
        kr = sb("kr", [P, RING * S], BF16)
        qr = sb("qr", [P, RING * S], BF16)
        pr = sb("pr", [P, PRING, GT], F32)
        v_all = sb("v_all", [P, NT, D], F32)
        vst = [sb(f"vst{i}", [P, KB - QUAD, VC], F32) for i in range(2)]
        vtail = sb("vtail", [P, QUAD, VC], F32)
        oT = sb("oT", [P, GT], F32)
        mx = sb("mx", [P, TPG, MAXU], F32)
        nm = sb("nm", [P, TPG], F32)
        nmp = sb("nmp", [P, TPG, 2], BF16)
        osum = sb("osum", [P, TPG, HD + 1], F32)
        rden = sb("rden", [P, TPG], F32)
        sc = [pb(f"sc{i}", [P, MAXW], F32) for i in range(2)]
        st = [pb(f"st{i}", [P, GT], F32) for i in range(2)]
        pv = pb("pv", [P, GT], F32)
        post = pb("post", [P, GT], F32)

        loaded = [sem(f"loaded{i}") for i in range(2)]
        v_loaded = sem("v_loaded")
        v_cols = sem("v_columns_set")
        ones_set = sem("ones_set")
        sc_full = sem("sc_full")
        sc_read = sem("sc_read")
        nmp_ready = sem("nmp_ready")
        mt_full = sem("mt_full")
        m_rows = sem("m_rows")
        st_full = sem("st_full")
        exp_done = sem("exp_done")
        pv_done = sem("pv_done")
        pv_read = sem("pv_read")
        o_full = sem("o_full")
        o_read = sem("o_read")
        v_ready = sem("v_ready")
        vt_ready = sem("vt_ready")
        passed = sem("passed_a")
        max_chain, out_chain = sem("max_chain"), sem("out_chain")
        LOADS = 2 * len(PAIRS)

        block = ctx.enter_context(nc.Block())

        def rolled(engine, slot):
            slot(0, 0, 0, False, False, True)
            with engine.Fori(1, QB) as qb:
                slot(0, qb, 0, True, True, True)
            with engine.Fori(0, HEADS // 2 - 1) as i:
                with engine.Fori(0, QB) as qb:
                    slot(2 * i + 1, qb, 1, True, True, True)
                with engine.Fori(0, QB) as qb:
                    slot(2 * i + 2, qb, 0, True, True, True)
            slot(HEADS - 1, 0, 1, True, True, False)
            with engine.Fori(1, QB) as qb:
                slot(HEADS - 1, qb, 1, True, False, False)

        def ring(stage):
            return (stage % RING) * S

        @block.sync
        def _(sp):
            def load(n, par):
                h, tok = n % H, (n // H) * S
                for w, dst in ((0, qr), (1, kr)):
                    for i, pair in enumerate(PAIRS):
                        sp.dma_start(dst[i * HD:(i + 1) * HD, bass.ds(ring(n), S)],
                                     c.parts_d[w, pair[w], bass.ds(h * HD, HD), bass.ds(tok, S)]).then_inc(loaded[par], DMA)

            def reload(n, par):
                wait_alone(sp, st_full, (n - RING + 1) * QB * KB, passed)
                load(n, par)

            load(0, 0)
            sp.dma_start(v_all[:, :, :], c.v_d.rearrange("(t p) d -> p t d", p=P)).then_inc(v_loaded, DMA)
            load(1, 1)
            sp.wait_ge(loaded[0], LOADS * DMA)
            load(2, 0)
            with sp.Fori(0, (HEADS - RING - 1) // 2) as i:
                reload(2 * i + RING, 1)
                reload(2 * i + RING + 1, 0)
            reload(HEADS - 1, 1)

        @block.gpsimd
        def _(pool):
            def v_of(n, k0, k1):
                return v_all[:, bass.ds((n // H) * KB + k0, k1 - k0), bass.ds((n % H) * HD, HD)]

            def tail(n):
                nc.gpsimd.tensor_copy(vtail[:, :, 0:HD], v_of(n, KB - QUAD, KB)).then_inc(vt_ready, 1)

            def main(n, par):
                nc.gpsimd.tensor_copy(vst[par][:, :, 0:HD], v_of(n, 0, KB - QUAD)).then_inc(v_ready, 1)

            for v in (vst[0], vst[1], vtail):
                nc.gpsimd.memset(v[:, :, HD:HD + 1], 1.0).then_inc(v_cols, 1)
                nc.gpsimd.memset(v[:, :, HD + 1:VC], 0.0).then_inc(v_cols, 1)
            pool.wait_ge(v_loaded, DMA)
            main(0, 0)
            tail(0)
            main(1, 1)

            def stage(n, par):
                wait_alone(pool, pv_done, n * QB * QUADS + 2, passed)
                tail(n)
                main(n + 1, 1 - par)

            with pool.Fori(0, HEADS // 2 - 1) as i:
                stage(2 * i + 1, 1)
                stage(2 * i + 2, 0)
            pool.wait_ge(pv_done, (HEADS - 1) * QB * QUADS + 2)
            tail(HEADS - 1)

        @block.tensor
        def _(pe):
            def max_unit(stage, qb, u):
                t, k = divmod(u, MAXU)
                n = (stage * QB + qb) * UNITS + u
                pe.wait_ge(sc_read, n + 1)
                for j in range(MAXW // GT):
                    last = nc.tensor.matmul(sc[u % 2][:, j * GT:(j + 1) * GT],
                                            qr[0:ROWS, bass.ds(ring(stage) + qb * GT + t * P, P)],
                                            kr[0:ROWS, bass.ds(ring(stage) + k * MAXW + j * GT, GT)], start=True, stop=True)
                last.then_inc(sc_full, 1)

            def max_rows(n):
                pe.wait_ge(nmp_ready, n + 1)
                for t in range(TPG):
                    last = nc.tensor.matmul(post[ROWS:ROWSM, t * P:(t + 1) * P], nmp[:, t, :], c.identb[:, :], start=True, stop=True)
                last.then_inc(mt_full, 1)

            def scores(stage, qb, kb):
                n = (stage * QB + qb) * KB + kb
                pe.wait_ge(exp_done, n + 1)
                nc.tensor.matmul(st[kb % 2][:, :], kr[0:ROWSM, bass.ds(ring(stage) + kb * P, P)],
                                 qr[0:ROWSM, bass.ds(ring(stage) + qb * GT, GT)], start=True, stop=True).then_inc(st_full, 1)

            def times_v(quad, v, exps):
                pe.wait_ge(exp_done, exps + 2)
                for j in range(QUAD):
                    last = nc.tensor.matmul(pv[VC * j:VC * (j + 1), :], v[:, j, :], pr[:, (quad % 2) * QUAD + j, :],
                                            start=(quad == 0), stop=(quad == QUADS - 1))
                last.then_inc(pv_done, 1)

            def out_back(s):
                pe.wait_ge(pv_read, s + 1)
                for t in range(TPG):
                    last = nc.tensor.transpose(post[:, t * P:(t + 1) * P], oT[:, t * P:(t + 1) * P], c.ident[:, :])
                last.then_inc(o_full, 1)

            pe.sem_inc(pv_done, 2)
            pe.wait_ge(v_cols, 6)
            pe.wait_ge(ones_set, 1)
            pe.wait_ge(loaded[0], LOADS * DMA)
            with pe.Fori(0, QB) as qb:
                for u in range(UNITS):
                    max_unit(0, qb, u)
                max_rows(qb)

            def slot(stage, qb, par, pending_out, pending_max, maxima):
                s = stage * QB + qb
                pe.wait_ge(m_rows, s + 1)
                if maxima:
                    pe.wait_ge(loaded[1 - par], ((stage + 1) // 2 + 1) * LOADS * DMA)
                for quad in range(QUADS):
                    scores(stage, qb, 4 * quad)
                    scores(stage, qb, 4 * quad + 1)
                    if maxima:
                        max_unit(stage + 1, qb, 2 * quad)
                        max_unit(stage + 1, qb, 2 * quad + 1)
                    scores(stage, qb, 4 * quad + 2)
                    scores(stage, qb, 4 * quad + 3)
                    if quad == 0 and pending_out:
                        pe.wait_ge(vt_ready, (s - 1) // QB + 1)
                        times_v(QUADS - 1, vtail, s * KB)
                    if quad == 1:
                        pe.wait_ge(v_ready, stage + 1)
                        if pending_out:
                            pe.wait_ge(pv_read, s)
                    if quad:
                        times_v(quad - 1, vst[par][:, (quad - 1) * QUAD:quad * QUAD, :], s * KB + quad * QUAD)
                    if quad == 2 and pending_out:
                        if pending_max:
                            pe.wait_ge(m_rows, s + QB - 1)
                        else:
                            pe.wait_ge(m_rows, HEADS * QB)
                            pe.wait_ge(o_read, s - 1)
                        out_back(s - 1)
                    if quad == 4 and pending_max:
                        pe.wait_ge(o_read, s)
                        max_rows(s + QB - 1)

            rolled(pe, slot)
            pe.wait_ge(vt_ready, HEADS)
            times_v(QUADS - 1, vtail, HEADS * QB * KB)
            pe.wait_ge(o_read, HEADS * QB - 1)
            out_back(HEADS * QB - 1)

        @block.scalar
        def _(act):
            act.sem_inc(exp_done, 2)

            def sums_read(s):
                act.wait_ge(pv_done, (s + 1) * QUADS + 2)
                nc.scalar.activation(oT[:, :], pv[:, :], ACT.Identity).then_inc(pv_read, 1)

            def slot(stage, qb, par, pending_out, pending_max, maxima):
                s = stage * QB + qb
                for kb in range(KB):
                    if kb % QUAD == 0:
                        act.wait_ge(pv_done, s * QUADS + kb // QUAD + 1)
                    act.wait_ge(st_full, s * KB + kb + 1)
                    nc.scalar.activation(pr[:, kb % PRING, :], st[kb % 2][:, :], ACT.Exp).then_inc(exp_done, 1)
                    if kb == QUAD and pending_out:
                        sums_read(s - 1)

            rolled(act, slot)
            sums_read(HEADS * QB - 1)

        @block.vector
        def _(dve):
            dve.sem_inc(sc_read, 2)
            dve.sem_inc(out_chain, 1)
            nc.vector.memset(kr[ROWS:ROWSM, :], 1.0).then_inc(ones_set, 1)

            def step(instruction, s, value):
                instruction.then_inc(s, 1)
                dve.wait_ge(s, value)

            def max_unit(n, u):
                dve.wait_ge(sc_full, n * UNITS + u + 1)
                nc.vector.reduce_max(mx[:, u // MAXU, u % MAXU:u % MAXU + 1], sc[u % 2][:, :], AX.X).then_inc(sc_read, 1)

            def maxima_done(n):
                dve.wait_ge(sc_read, (n + 1) * UNITS + 2)
                step(nc.vector.tensor_reduce(nm[:, :], mx[:, :, :], AX.X, ALU.max, negate=True), max_chain, 2 * n + 1)
                step(nc.vector.tensor_copy(nmp[:, :, 0], nm[:, :]), max_chain, 2 * n + 2)
                nc.vector.tensor_tensor(nmp[:, :, 1], nm[:, :], nmp[:, :, 0], ALU.subtract).then_inc(nmp_ready, 1)

            def rows_kept(n):
                dve.wait_ge(mt_full, n + 1)
                nc.vector.tensor_copy(qr[ROWS:ROWSM, bass.ds(ring(n // QB) + (n % QB) * GT, GT)],
                                      post[ROWS:ROWSM, :]).then_inc(m_rows, 1)

            def output_kept(s):
                stage, qb = s // QB, s % QB
                dve.wait_ge(out_chain, 2 * s + 1)
                dve.wait_ge(o_full, s + 1)
                o = post[:, :].rearrange("p (t j v) -> p t v j", t=TPG, v=VC)[:, :, 0:HD + 1, :]
                step(nc.vector.tensor_reduce(osum[:, :, :], o, AX.X, ALU.add), o_read, s + 1)
                step(nc.vector.reciprocal(rden[:, :], osum[:, :, HD]), out_chain, 2 * s + 2)
                nc.vector.tensor_tensor(c.attn[:, bass.ds((stage // H) * KB + qb * TPG, TPG), bass.ds((stage % H) * HD, HD)],
                                        osum[:, :, 0:HD], rden[:, :].unsqueeze(2).broadcast_to([P, TPG, HD]),
                                        ALU.mult).then_inc(out_chain, 1)

            with dve.Fori(0, QB) as qb:
                for u in range(UNITS):
                    max_unit(qb, u)
                maxima_done(qb)
                rows_kept(qb)

            def slot(stage, qb, par, pending_out, pending_max, maxima):
                s = stage * QB + qb
                for quad in range(QUADS):
                    if maxima:
                        max_unit(s + QB, 2 * quad)
                        max_unit(s + QB, 2 * quad + 1)
                    if quad == 2 and pending_out:
                        output_kept(s - 1)
                    if quad == 4 and pending_max:
                        rows_kept(s + QB - 1)
                if maxima:
                    maxima_done(s + QB)

            rolled(dve, slot)
            output_kept(HEADS * QB - 1)


def output_phase(nc, a, c):
    with ExitStack() as ctx:
        sb, pb, sem = tools(nc, ctx)
        base = [sb(f"o_base{i}", [P, TPG, D], F32) for i in range(2)]
        att = [sb(f"att{i}", [P, TPG, D], F32) for i in range(2)]
        attT = [sb(f"attT{i}", [P, KC, GT], F32) for i in range(2)]
        tp = [[pb(f"tp{i}{k}", [P, GT], F32) for k in range(KC)] for i in range(2)]
        ob = [[pb(f"ob{i}{k}", [P, 2, D], F32) for k in range(2)] for i in range(2)]
        passed = sem("passed_o")
        base_in = [sem(f"base_in{i}") for i in range(2)]
        stored = [sem(f"stored{i}") for i in range(2)]
        att_ready = sem("att_ready")
        tp_full = sem("tp_full")
        attT_ready = sem("attT_ready")
        ob_full = sem("ob_full")
        sum_ready = sem("sum_ready")
        block = ctx.enter_context(nc.Block())

        def tokens_of(dram, g):
            return dram[bass.ds(g * GT, GT), :].rearrange("(t p) d -> p t d", p=P)

        def rolled(engine, body):
            with engine.Fori(0, NG // 2 - 1) as gg:
                body(2 * gg, 0, True)
                body(2 * gg + 1, 1, True)
            body(NG - 2, 0, True)
            body(NG - 1, 1, False)

        @block.sync
        def _(sp):
            def load(g, par):
                wait_alone(sp, stored[par], (g // 2 + 1) * DMA, passed)
                sp.dma_start(base[par][:, :, :], tokens_of(c.base_d, g)).then_inc(base_in[par], DMA)

            def body(g, par, more):
                if more:
                    load(g + 1, 1 - par)
                wait_alone(sp, sum_ready, g + 1 + 2, passed)
                sp.dma_start(tokens_of(a["out"], g), base[par][:, :, :]).then_inc(stored[par], DMA)

            sp.sem_inc(stored[0], DMA)
            sp.sem_inc(stored[1], DMA)
            load(0, 0)
            rolled(sp, body)
            for i in range(2):
                sp.wait_ge(stored[i], (NG // 2 + 1) * DMA)

        @block.gpsimd
        def _(pool):
            def body(g, par, more):
                wait_alone(pool, attT_ready, g * KC + 2, passed)
                nc.gpsimd.tensor_copy(att[par][:, :, :], c.attn[:, bass.ds(g * TPG, TPG), :]).then_inc(att_ready, 1)

            rolled(pool, body)

        @block.tensor
        def _(pe):
            def turn(g, par):
                pe.wait_ge(att_ready, g + 1)
                for k in range(KC):
                    pe.wait_ge(attT_ready, g * KC + k + 1)
                    for t in range(TPG):
                        last = nc.tensor.transpose(tp[par][k][:, t * P:(t + 1) * P], att[par][:, t, k * P:(k + 1) * P], c.ident[:, :])
                    last.then_inc(tp_full, 1)

            def body(g, par, more):
                if more:
                    turn(g + 1, 1 - par)
                pe.wait_ge(attT_ready, g * KC + KC + 4)
                pe.wait_ge(sum_ready, g + 1)
                for t in range(TPG):
                    for k in range(KC):
                        last = nc.tensor.matmul(ob[par][t // 2][:, t % 2, :], attT[par][:, k, t * P:(t + 1) * P], c.woT[:, k, :],
                                                start=(k == 0), stop=(k == KC - 1))
                last.then_inc(ob_full, 1)

            turn(0, 0)
            rolled(pe, body)

        @block.scalar
        def _(act):
            def body(g, par, more):
                for k in range(KC):
                    act.wait_ge(tp_full, g * KC + k + 1)
                    if k == 0:
                        act.wait_ge(sum_ready, g + 1)
                    nc.scalar.activation(attT[par][:, k, :], tp[par][k][:, :], ACT.Identity).then_inc(attT_ready, 1)

            act.sem_inc(attT_ready, 4)
            rolled(act, body)

        @block.vector
        def _(dve):
            def body(g, par, more):
                dve.wait_ge(ob_full, g + 1)
                dve.wait_ge(base_in[par], (g // 2 + 1) * DMA)
                for i in range(2):
                    ins = nc.vector.tensor_tensor(base[par][:, 2 * i:2 * i + 2, :], ob[par][i][:, :, :], base[par][:, 2 * i:2 * i + 2, :], ALU.add)
                ins.then_inc(sum_ready, 1)

            dve.sem_inc(sum_ready, 2)
            rolled(dve, body)


class Kept:
    pass


def layer(nc, x, Wq, bq, Wk, bk, Wv, bv, Wo, bo, Wg, Wu, Wd, Wr, temperature, out):
    a = {"x": x.rearrange("b s d -> (b s) d"), "Wq": Wq, "bq": bq, "Wk": Wk, "bk": bk, "Wv": Wv, "bv": bv, "Wo": Wo, "bo": bo,
         "Wg": Wg, "Wu": Wu, "Wd": Wd, "Wr": Wr, "temperature": temperature, "out": out.rearrange("b s d -> (b s) d")}
    c = Kept()
    c.parts_d = nc.dram_tensor("parts_d", (2, 3, D, TOK), BF16, kind="Internal").ap()
    c.base_d = nc.dram_tensor("base_d", (TOK, D), F32, kind="Internal").ap()
    c.v_d = nc.dram_tensor("v_d", (TOK, D), F32, kind="Internal").ap()
    with ExitStack() as ctx:
        sb, _, _ = tools(nc, ctx)
        c.ident = sb("ident", [P, P], F32)
        c.identb = sb("identb", [P, P], BF16)
        c.woT = sb("woT", [P, KC, D], F32)
        with ExitStack() as early_ctx:
            sb, _, _ = tools(nc, early_ctx)
            c.experts = [sb(f"experts{hl}", [P, 3, E, KC, FI], F32R) for hl in range(2)]
            c.wT = [[sb(f"wT{n}{hl}", [P, KC, D], F32R) for hl in range(2)] for n in range(3)]
            c.wr = [sb(f"wr{hl}", [P, KC, E], F32R) for hl in range(2)]
            c.before = sb("before", [P, E, E], F32)
            c.bk, c.bqs = (sb(n, [P, KC], F32) for n in ("bk", "bqs"))
            c.bv, c.bo = sb("bv", [P, D], F32), sb("bo", [P, D], F32)
            c.rtemp, c.eps = (sb(n, [P, 1], F32) for n in ("rtemp", "eps"))
            setup_phase(nc, a, c)
            token_phase(nc, a, c)
        c.attn = ctx.enter_context(nc.sbuf_tensor("attn", [P, NT, D], F32))
        attention_phase(nc, a, c)
        output_phase(nc, a, c)


_INS = ["L0_attn_hidden_states", "L0_attn_Wq", "L0_attn_bq", "L0_attn_Wk", "L0_attn_bk", "L0_attn_Wv", "L0_attn_bv", "L0_attn_Wo",
        "L0_attn_bo", "L0_ffn_Wg", "L0_ffn_Wu", "L0_ffn_Wd", "L0_ffn_Wr", "L0_ffn_temperature"]


def kernel(**inputs):
    import numpy as _np
    import concourse.bacc as _bacc
    from concourse.bass_utils import run_bass_kernel_spmd as _run

    nc = _bacc.Bacc("TRN2", target_bir_lowering=False, num_devices=1)
    arrays, args = {}, []
    for name in _INS:
        arr = _np.ascontiguousarray(inputs[name])
        arrays[f"in_{name}"] = arr
        args.append(nc.dram_tensor(f"in_{name}", arr.shape, mybir.dt.from_np(arr.dtype), kind="ExternalInput").ap())
    args.append(nc.dram_tensor("out_0", (B, S, D), F32, kind="ExternalOutput").ap())
    layer(nc, *args)
    return _run(nc, [arrays], core_ids=[0]).results[0]["out_0"]
```

```python
import concourse.bass as bass
from concourse import mybir
from contextlib import ExitStack

F32 = mybir.dt.float32
BF16 = mybir.dt.bfloat16
F32R = mybir.dt.float32r
ALU = mybir.AluOpType
ACT = mybir.ActivationFunctionType
AX = mybir.AxisListType

P = 128
B, S, D = 2, 4096, 256
H, HD = 16, 16
E, FI = 8, 256
TOK = B * S
KC = D // P
GT = 512
NG = TOK // GT
TPG = GT // P
NT = TOK // P
HEADS = B * H
QB = S // GT
KB = S // P
QUAD = 4
QUADS = KB // QUAD
MAXW = 1024
MAXU = S // MAXW
UNITS = TPG * MAXU
PAIRS = ((0, 0), (0, 1), (1, 0), (1, 1), (0, 2), (2, 0))
ROWS = len(PAIRS) * HD
ROWSM = ROWS + 2
VC = 32
PRING = 2 * QUAD
SCALE = HD ** -0.5
EPS = 1e-5
CENTER, LOWER, UPPER = 0.36787944117144233, 0.5 - 0.28768207245178085, 0.5
TINY = 1e-8
DMA = 16


def tools(nc, ctx):
    def sb(name, shape, dt):
        return ctx.enter_context(nc.sbuf_tensor(name, shape, dt))

    def pb(name, shape, dt):
        return ctx.enter_context(nc.psum_tensor(name, shape, dt))

    def sem(name):
        return ctx.enter_context(nc.semaphore(name))

    return sb, pb, sem


def wait_alone(engine, sem, value, passed):
    engine.wait_ge(sem, value)
    engine.sem_inc(passed, 1)


def product(nc, out, lhs, rhs, low_low=False):
    terms = [(a, b) for k in range(len(lhs)) for a, b in ((0, 0), (0, 1), (1, 0)) + (((1, 1),) if low_low else ())]
    terms = [(k, a, b) for k in range(len(lhs)) for a, b in terms[:len(terms) // len(lhs)]]
    for n, (k, a, b) in enumerate(terms):
        last = nc.tensor.matmul(out, lhs[k][a], rhs[k][b], start=(n == 0), stop=(n == len(terms) - 1))
    return last


def setup_phase(nc, a, c):
    with ExitStack() as ctx:
        sb, pb, sem = tools(nc, ctx)
        wnat = sb("wnat", [P, 4, KC, D], F32)
        raw = [sb(f"raw{n}", [P, E, KC, FI], F32) for n in range(3)]
        wr = sb("wr", [P, KC, E], F32)
        bq, temp = sb("bq", [P, KC], F32), sb("temp", [P, 1], F32)
        psT = [pb(f"psT{i}", [P, 512], F32) for i in range(2)]
        s_w = sem("w_loaded")
        s_raw = [sem(f"experts_loaded{n}") for n in range(3)]
        s_zero = sem("zeroed")
        s_id = sem("identity_ready")
        s_const = sem("constants_ready")
        s_t = sem("weight_transposed")
        s_high = sem("high_ready")
        s_low = sem("low_ready")
        s_ehigh = sem("expert_high_ready")
        s_small = sem("small_loaded")
        block = ctx.enter_context(nc.Block())

        @block.sync
        def _(sp):
            for n, name in enumerate(("Wq", "Wk", "Wv", "Wo")):
                sp.dma_start(wnat[:, n, :, :], a[name].rearrange("(c p) i -> p c i", p=P)).then_inc(s_w, DMA)
            sp.dma_start(bq[:, :], a["bq"].rearrange("(c p) -> p c", p=P), allow_slow_non_contiguous=True).then_inc(s_small, DMA)
            sp.dma_start(c.bk[:, :], a["bk"].rearrange("(c p) -> p c", p=P), allow_slow_non_contiguous=True).then_inc(s_small, DMA)
            sp.dma_start(c.bv[:, :], a["bv"].partition_broadcast(P)).then_inc(s_small, DMA)
            sp.dma_start(c.bo[:, :], a["bo"].partition_broadcast(P)).then_inc(s_small, DMA)
            sp.dma_start(temp[:, :], a["temperature"].partition_broadcast(P)).then_inc(s_small, DMA)
            sp.dma_start(wr[:, :, :], a["Wr"].rearrange("(c p) e -> p c e", p=P)).then_inc(s_small, DMA)
            for n, name in enumerate(("Wg", "Wu", "Wd")):
                sp.dma_start(raw[n][:, :, :, :], a[name].rearrange("e (c p) i -> p e c i", p=P)).then_inc(s_raw[n], DMA)

        @block.gpsimd
        def _(pool):
            nc.gpsimd.memset(c.ident[:, :], 0.0).then_inc(s_zero, 1)
            nc.gpsimd.memset(c.before[:, :, :], 1.0).then_inc(s_zero, 1)
            pool.wait_ge(s_zero, 2)
            nc.gpsimd.affine_select(out=c.ident[:, :], in_=c.ident[:, :], compare_op=ALU.not_equal, fill=1.0,
                                    base=0, pattern=[[-1, P]], channel_multiplier=1).then_inc(s_id, 1)
            nc.gpsimd.affine_select(out=c.before[:, :, :], in_=c.before[:, :, :], compare_op=ALU.is_gt, fill=0.0,
                                    base=0, pattern=[[1, E], [-1, E]], channel_multiplier=0).then_inc(s_id, 1)
            pool.wait_ge(s_ehigh, 3 * 2)
            nc.gpsimd.tensor_tensor(c.experts[1][:, 2, E - 2:, :, :], raw[2][:, E - 2:, :, :], c.experts[0][:, 2, E - 2:, :, :], ALU.subtract).then_inc(s_id, 1)

        @block.tensor
        def _(pe):
            pe.wait_ge(s_id, 1)
            pe.wait_ge(s_w, 4 * DMA)
            for n in range(4):
                for i in range(KC):
                    u = KC * n + i
                    if u >= 2:
                        pe.wait_ge(s_low, u - 1)
                    for o in range(KC):
                        last = nc.tensor.transpose(psT[u % 2][:, o * P:(o + 1) * P], wnat[:, n, o, i * P:(i + 1) * P], c.ident[:, :])
                    last.then_inc(s_t, 1)

        @block.scalar
        def _(act):
            for u in range(4 * KC):
                act.wait_ge(s_t, u + 1)
                nc.scalar.activation(c.wT[u // KC][0][:, u % KC, :], psT[u % 2][:, 0:D], ACT.Identity).then_inc(s_high, 1)
            for n in range(3):
                act.wait_ge(s_raw[n], DMA)
                for e0 in (0, E // 2):
                    nc.scalar.activation(c.experts[0][:, n, e0:e0 + E // 2, :, :], raw[n][:, e0:e0 + E // 2, :, :], ACT.Identity).then_inc(s_ehigh, 1)

        @block.vector
        def _(dve):
            for n in range(4):
                for i in range(KC):
                    u = KC * n + i
                    dve.wait_ge(s_high, u + 1)
                    nc.vector.tensor_tensor(c.wT[n][1][:, i, :], psT[u % 2][:, 0:D], c.wT[n][0][:, i, :], ALU.subtract).then_inc(s_low, 1)
            dve.wait_ge(s_id, 1)
            nc.vector.tensor_copy(c.identb[:, :], c.ident[:, :]).then_inc(s_const, 1)
            nc.vector.memset(c.eps[:, :], EPS).then_inc(s_const, 1)
            dve.wait_ge(s_small, 6 * DMA)
            nc.vector.tensor_scalar(c.bqs[:, :], bq[:, :], SCALE, None, ALU.mult).then_inc(s_const, 1)
            nc.vector.reciprocal(c.rtemp[:, :], temp[:, :]).then_inc(s_const, 1)
            nc.vector.tensor_copy(c.wr[0][:, :, :], wr[:, :, :]).then_inc(s_const, 1)
            dve.wait_ge(s_const, 5)
            nc.vector.tensor_tensor(c.wr[1][:, :, :], wr[:, :, :], c.wr[0][:, :, :], ALU.subtract).then_inc(s_const, 1)
            for n in range(3):
                for half, e0 in enumerate((0, E // 2)):
                    e1 = E - 2 if n == 2 and e0 else e0 + E // 2
                    dve.wait_ge(s_ehigh, 2 * n + half + 1)
                    nc.vector.tensor_tensor(c.experts[1][:, n, e0:e1, :, :], raw[n][:, e0:e1, :, :], c.experts[0][:, n, e0:e1, :, :],
                                            ALU.subtract).then_inc(s_const, 1)


MISC = (("x", 0, "dve"), ("x", 1, "dve"), ("route", 0, "dve"), ("q", 0, "act"), ("q", 1, "act"),
        ("k", 0, "act"), ("k", 1, "act"), ("v", 0, "dve"), ("v", 1, "dve"))
MISC_AFTER = {1: (0, 1), 2: (2,), 3: (3, 4), 5: (5, 6), 7: (7, 8)}
MISC_ACT = sum(m[2] == "act" for m in MISC)
MISC_DVE = len(MISC) - MISC_ACT
SPLITS = 2 * KC
LINKS = 25


def emptied(n):
    return sum(m[2] == MISC[n][2] for m in MISC[:n + 1])


def token_phase(nc, a, c):
    with ExitStack() as ctx:
        sb, pb, sem = tools(nc, ctx)
        x_in = [sb(f"x_in{i}", [P, TPG, D], F32) for i in range(2)]
        base = [sb(f"base{i}", [P, TPG, D], F32) for i in range(2)]
        xn = sb("xn", [P, TPG, D], F32)
        xT = [[sb(f"xT{i}{hl}", [P, KC, GT], F32R) for hl in range(2)] for i in range(2)]
        full = [sb(f"full{i}", [P, GT], F32) for i in range(2)]
        rest = [sb(f"rest{i}", [P, GT], F32) for i in range(2)]
        part = [sb(f"part{i}", [P, 3, GT], BF16) for i in range(2)]
        gated = [sb(f"gated{i}", [P, GT], F32) for i in range(2)]
        hraw = [sb(f"hraw{i}", [P, GT], F32) for i in range(2)]
        hid = [[sb(f"hid{i}{hl}", [P, KC, GT], F32R) for hl in range(2)] for i in range(2)]
        v_sb = [sb(f"v_sb{i}", [P, 2, D], F32) for i in range(2)]
        stats = sb("stats", [P, TPG, 6], F32)
        mv = sb("mv", [P, TPG, 2], F32)
        std = sb("std", [P, TPG], F32)
        rstd = sb("rstd", [P, TPG], F32)
        rt = sb("rt", [P, 10, TPG, E], F32)
        rs = sb("rs", [P, 6, TPG], F32)
        beats = sb("beats", [P, 2, TPG, E, E], F32)
        wts = [sb(f"wts{i}", [P, TPG, E], F32) for i in range(2)]
        misc = [pb(f"misc{i}", [P, 512], F32) for i in range(2)]
        gate = [pb(f"gate{i}", [P, GT], F32) for i in range(2)]
        up = [pb(f"up{i}", [P, GT], F32) for i in range(2)]
        down = [pb(f"down{i}", [P, 2, D], F32) for i in range(2)]

        x_loaded = [sem(f"x_loaded{i}") for i in range(2)]
        stats_done = sem("stats_done")
        std_done = sem("std_done")
        xn_done = sem("xn_done")
        xh_ready = sem("xT_high_ready")
        misc_full = sem("misc_full")
        misc_act = sem("misc_act")
        misc_dve = sem("misc_dve")
        dist_ready = sem("dist_ready")
        exp_given = sem("exp_given")
        rest_ready = sem("rest_ready")
        second_ready = sem("second_ready")
        parts_ready = sem("parts_ready")
        parts_stored = [sem(f"parts_stored{i}") for i in range(2)]
        gu_full = sem("gate_up_full")
        silu_done = sem("silu_done")
        hid_ready = sem("hid_ready")
        hh_ready = sem("hid_high_ready")
        hl_ready = sem("hid_low_ready")
        v_stored = [sem(f"v_stored{i}") for i in range(2)]
        down_full = sem("down_full")
        down_used = sem("down_used")
        base_init = sem("base_init")
        base_stored = [sem(f"base_stored{i}") for i in range(2)]
        vchain = sem("vector_chain")
        passed = sem("passed")

        block = ctx.enter_context(nc.Block())

        def rolled(engine, before, body):
            before()
            with engine.Fori(0, NG // 2 - 1) as gg:
                body(2 * gg, 0, False, True)
                body(2 * gg + 1, 1, False, True)
            body(NG - 2, 0, False, False)
            body(NG - 1, 1, True, False)

        def tokens_of(dram, g):
            return dram[bass.ds(g * GT, GT), :].rearrange("(t p) d -> p t d", p=P)

        @block.sync
        def _(sp):
            def load(g, par):
                sp.dma_start(x_in[par][:, :, :], tokens_of(a["x"], g)).then_inc(x_loaded[par], DMA)

            def store_parts(g):
                for u in range(SPLITS):
                    w, half = divmod(u, KC)
                    wait_alone(sp, parts_ready, g * SPLITS + u + 1 + 2, passed)
                    sp.dma_start(c.parts_d[w, :, half * P:(half + 1) * P, bass.ds(g * GT, GT)].rearrange("r p t -> p r t"),
                                 part[u % 2][:, :, :]).then_inc(parts_stored[u % 2], DMA)

            def store_v(g):
                for i in range(2):
                    wait_alone(sp, misc_dve, g * MISC_DVE + emptied(len(MISC) - 2 + i), passed)
                    sp.dma_start(c.v_d[bass.ds(g * GT + 2 * i * P, 2 * P), :].rearrange("(t p) d -> p t d", p=P),
                                 v_sb[i][:, :, :]).then_inc(v_stored[i], DMA)

            def before():
                for i in range(2):
                    sp.sem_inc(base_stored[i], DMA)
                    sp.sem_inc(parts_stored[i], DMA)
                    sp.sem_inc(v_stored[i], DMA)
                load(0, 0)
                load(1, 1)
                store_parts(0)
                store_v(0)

            def body(g, par, last, more):
                if more:
                    sp.wait_ge(xn_done, g + 1)
                    wait_alone(sp, base_init, g + 1, passed)
                    load(g + 2, par)
                if not last:
                    store_parts(g + 1)
                    store_v(g + 1)
                wait_alone(sp, down_used, (g + 1) * E * 2 + 2, passed)
                sp.dma_start(tokens_of(c.base_d, g), base[par][:, :, :]).then_inc(base_stored[par], DMA)

            rolled(sp, before, body)
            for i in range(2):
                sp.wait_ge(base_stored[i], (NG // 2 + 1) * DMA)
                sp.wait_ge(parts_stored[i], (SPLITS // 2 * NG + 1) * DMA)
                sp.wait_ge(v_stored[i], (NG + 1) * DMA)

        def pieces(pair, c0=0, cols=None):
            return [[v[:, k, c0:c0 + cols if cols else None] for v in pair] for k in range(KC)]

        def tile_of(pair, t):
            return pieces(pair, t * P, P)

        @block.tensor
        def _(pe):
            def misc_unit(g, par, n, first):
                kind, i, _ = MISC[n]
                if n >= 2:
                    prev = n - 2
                    pe.wait_ge(misc_act if MISC[prev][2] == "act" else misc_dve,
                               g * (MISC_ACT if MISC[prev][2] == "act" else MISC_DVE) + emptied(prev))
                elif not first:
                    pe.wait_ge(misc_dve, (g - 1) * MISC_DVE + emptied(len(MISC) - 2 + n))
                bank = misc[(par * len(MISC) + n) % 2]
                if kind == "x":
                    pe.wait_ge(xn_done, g + 1)
                    for t in range(TPG):
                        last = nc.tensor.transpose(bank[:, t * P:(t + 1) * P], xn[:, t, i * P:(i + 1) * P], c.ident[:, :])
                elif kind == "route":
                    pe.wait_ge(misc_dve, g * MISC_DVE + KC)
                    for t in range(TPG):
                        last = product(nc, bank[:, t * E:(t + 1) * E], tile_of(xT[par], t), pieces(c.wr), low_low=True)
                elif kind in "qk":
                    last = product(nc, bank[:, :], pieces(c.wT["qk".index(kind)], i * P, P), pieces(xT[par]))
                else:
                    for j in range(2):
                        last = product(nc, bank[:, j * D:(j + 1) * D], tile_of(xT[par], 2 * i + j), pieces(c.wT[2]))
                last.then_inc(misc_full, 1)

            def expert(w, e, c0, cols):
                return [[v[:, w, e, k, c0:c0 + cols] for v in c.experts] for k in range(KC)]

            def gate_up(g, par, e):
                for half in range(KC):
                    pe.wait_ge(hid_ready, (g * E + e) * KC + half + 1)
                    for w, bank in ((0, gate[half]), (1, up[half])):
                        last = product(nc, bank[:, :], expert(w, e, half * P, P), pieces(xT[par]))
                    last.then_inc(gu_full, 1)

            def down_proj(g, e):
                idx = g * E + e
                pe.wait_ge(hl_ready, idx * KC + KC + 2)
                for hf in range(2):
                    pe.wait_ge(down_used, idx * 2 + hf + 1)
                    for j in range(2):
                        t = 2 * hf + j
                        last = product(nc, down[hf][:, j, :], tile_of(hid[e % 2], t), expert(2, e, 0, D))
                    last.then_inc(down_full, 1)

            def before():
                for n in range(len(MISC)):
                    misc_unit(0, 0, n, True)

            def body(g, par, last, more):
                for e in range(E):
                    gate_up(g, par, e)
                    if e:
                        down_proj(g, e - 1)
                    if not last:
                        for n in MISC_AFTER.get(e, ()):
                            misc_unit(g + 1, 1 - par, n, False)
                down_proj(g, E - 1)

            rolled(pe, before, body)

        @block.scalar
        def _(act):
            def root(g):
                act.wait_ge(stats_done, g + 1)
                nc.scalar.activation(std[:, :], mv[:, :, 1], ACT.Sqrt, bias=c.eps[:, 0:1]).then_inc(std_done, 1)

            def misc_unit(g, par, n):
                kind, i, _ = MISC[n]
                if kind == "route":
                    act.wait_ge(misc_dve, g * MISC_DVE + emptied(n))
                    nc.scalar.activation(rt[:, 1, :, :], rt[:, 0, :, :], ACT.Exp, scale=-1.0).then_inc(exp_given, 1)
                    act.wait_ge(dist_ready, g + 1)
                    nc.scalar.activation(rt[:, 6, :, :], rt[:, 5, :, :], ACT.Exp, scale=-1.0 / 0.1).then_inc(exp_given, 1)
                    nc.scalar.activation(rt[:, 7, :, :], rt[:, 5, :, :], ACT.Exp, scale=-1.0 / 0.3).then_inc(exp_given, 1)
                    return
                if kind == "v":
                    return
                act.wait_ge(misc_full, g * len(MISC) + n + 1)
                bank = misc[(par * len(MISC) + n) % 2]
                if kind == "x":
                    nc.scalar.activation(xT[par][0][:, i, :], bank[:, :], ACT.Identity).then_inc(xh_ready, 1)
                    return
                u = (0 if kind == "q" else KC) + i
                bias, scale = (c.bqs, SCALE) if kind == "q" else (c.bk, 1.0)
                act.wait_ge(rest_ready, g * SPLITS + u + 1)
                nc.scalar.activation(full[u % 2][:, :], bank[:, :], ACT.Identity, bias=bias[:, i:i + 1], scale=scale)
                act.wait_ge(parts_stored[u % 2], (g * (SPLITS // 2) + u // 2 + 1) * DMA)
                nc.scalar.activation(part[u % 2][:, 0, :], bank[:, :], ACT.Identity, bias=bias[:, i:i + 1],
                                     scale=scale).then_inc(misc_act, 1)

            def before():
                root(0)
                for n in range(len(MISC)):
                    misc_unit(0, 0, n)

            def body(g, par, last, more):
                for e in range(E):
                    for half in range(KC):
                        act.wait_ge(gu_full, (g * E + e) * KC + half + 1)
                        nc.scalar.activation(gated[half][:, :], gate[half][:, :], ACT.Silu).then_inc(silu_done, 1)
                    for half in range(KC):
                        act.wait_ge(hid_ready, (g * E + e) * KC + half + 1 + 2)
                        nc.scalar.activation(hid[e % 2][0][:, half, :], hraw[half][:, :], ACT.Identity).then_inc(hh_ready, 1)
                    if not last:
                        if e == 0:
                            root(g + 1)
                        for n in MISC_AFTER.get(e, ()):
                            misc_unit(g + 1, 1 - par, n)

            rolled(act, before, body)

        @block.gpsimd
        def _(pool):
            def base_start(g, par):
                pool.wait_ge(x_loaded[par], (g // 2 + 1) * DMA)
                pool.wait_ge(base_stored[par], (g // 2 + 1) * DMA)
                for t in range(TPG):
                    ins = nc.gpsimd.tensor_tensor(base[par][:, t, :], x_in[par][:, t, :], c.bo[:, :], ALU.add)
                ins.then_inc(base_init, 1)

            def misc_unit(g, n):
                kind, i, _ = MISC[n]
                if kind in ("q", "k"):
                    u = (0 if kind == "q" else KC) + i
                    wait_alone(pool, rest_ready, g * SPLITS + u + 1 + 2, passed)
                    nc.gpsimd.tensor_copy(part[u % 2][:, 1, :], rest[u % 2][:, :]).then_inc(second_ready, 1)
                    pool.wait_ge(second_ready, g * SPLITS + u + 1)
                    nc.gpsimd.tensor_tensor(part[u % 2][:, 2, :], rest[u % 2][:, :], part[u % 2][:, 1, :],
                                            ALU.subtract).then_inc(parts_ready, 1)

            def before():
                pool.sem_inc(parts_ready, 2)
                pool.sem_inc(hl_ready, 2)
                base_start(0, 0)
                for n in range(len(MISC)):
                    misc_unit(0, n)

            def body(g, par, last, more):
                for e in range(E):
                    for half in range(KC):
                        pool.wait_ge(hh_ready, (g * E + e) * KC + half + 1)
                        nc.gpsimd.tensor_tensor(hid[e % 2][1][:, half, :], hraw[half][:, :], hid[e % 2][0][:, half, :],
                                                ALU.subtract).then_inc(hl_ready, 1)
                    if not last:
                        if e == 0:
                            base_start(g + 1, 1 - par)
                        for n in MISC_AFTER.get(e, ()):
                            misc_unit(g + 1, n)

            rolled(pool, before, body)

        @block.vector
        def _(dve):
            def step(instruction, s, value):
                instruction.then_inc(s, 1)
                dve.wait_ge(s, value)

            def norm(g, par, first):
                dve.wait_ge(x_loaded[par], (g // 2 + 1) * DMA)
                for t in range(TPG):
                    ins = nc.vector.bn_stats(stats[:, t, :], x_in[par][:, t, :])
                ins.then_inc(vchain, 1)
                wait_alone(dve, vchain, g * LINKS + 1, passed)
                for t in range(TPG):
                    ins = nc.vector.bn_aggr(mv[:, t, :], stats[:, t, :])
                ins.then_inc(stats_done, 1)
                dve.wait_ge(std_done, g + 1)
                step(nc.vector.reciprocal(rstd[:, :], std[:, :]), vchain, g * LINKS + 2)
                if not first:
                    dve.wait_ge(misc_dve, (g - 1) * MISC_DVE + KC)
                for t in range(TPG):
                    ins = nc.vector.tensor_scalar(xn[:, t, :], x_in[par][:, t, :], mv[:, t, 0:1], rstd[:, t:t + 1],
                                                  ALU.subtract, ALU.mult)
                ins.then_inc(xn_done, 1)

            def route(g, par, n):
                count = [2]

                def link(instruction):
                    count[0] += 1
                    step(instruction, vchain, g * LINKS + count[0])

                z, ez, den, inh, off, dist, w, fb, zone, rank = (rt[:, i, :, :] for i in range(10))
                wsum, none, some, fsum, total, rtotal = (rs[:, i, :] for i in range(6))

                def over(v):
                    return v.unsqueeze(2).broadcast_to([P, TPG, E])

                dve.wait_ge(misc_full, g * len(MISC) + n + 1)
                bank = misc[(par * len(MISC) + n) % 2]
                nc.vector.tensor_scalar(z, bank[:, 0:TPG * E].rearrange("p (t e) -> p t e", e=E), c.rtemp[:, 0:1], None,
                                        ALU.mult).then_inc(misc_dve, 1)
                dve.wait_ge(exp_given, g * 3 + 1)
                link(nc.vector.tensor_scalar(den, ez, 1.0, None, ALU.add))
                link(nc.vector.reciprocal(inh, den))
                link(nc.vector.tensor_scalar(off, inh, CENTER, None, ALU.subtract))
                nc.vector.scalar_tensor_tensor(out=dist, in0=off, scalar=-1.0, in1=off, op0=ALU.mult, op1=ALU.max).then_inc(dist_ready, 1)
                link(nc.vector.tensor_scalar(zone, inh, UPPER, None, ALU.is_le))
                link(nc.vector.scalar_tensor_tensor(out=zone, in0=inh, scalar=LOWER, in1=zone, op0=ALU.is_ge, op1=ALU.mult))
                dve.wait_ge(exp_given, g * 3 + 3)
                link(nc.vector.tensor_tensor(w, w, zone, ALU.mult))
                link(nc.vector.tensor_reduce(wsum, w, AX.X, ALU.add))
                link(nc.vector.tensor_scalar(none, wsum, TINY, None, ALU.is_lt))
                nc.vector.tensor_scalar(some, none, -1.0, 1.0, ALU.mult, ALU.add)
                for t in range(TPG):
                    mine = fb[:, t, :].unsqueeze(2).broadcast_to([P, E, E])
                    other = fb[:, t, :].unsqueeze(1).broadcast_to([P, E, E])
                    nc.vector.tensor_tensor(beats[:, 0, t, :, :], other, mine, ALU.is_gt)
                    ins = nc.vector.tensor_tensor(beats[:, 1, t, :, :], other, mine, ALU.is_ge)
                link(ins)
                for t in range(TPG):
                    ins = nc.vector.tensor_tensor(beats[:, 1, t, :, :], beats[:, 1, t, :, :], c.before[:, :, :], ALU.mult)
                link(ins)
                link(nc.vector.tensor_tensor(beats[:, 0, :, :, :], beats[:, 0, :, :, :], beats[:, 1, :, :, :], ALU.max))
                link(nc.vector.tensor_reduce(rank, beats[:, 0, :, :, :], AX.X, ALU.add))
                link(nc.vector.scalar_tensor_tensor(out=fb, in0=rank, scalar=2.0, in1=fb, op0=ALU.is_lt, op1=ALU.mult))
                link(nc.vector.tensor_reduce(fsum, fb, AX.X, ALU.add))
                link(nc.vector.tensor_scalar(fsum, fsum, TINY, None, ALU.max))
                link(nc.vector.reciprocal(total, fsum))
                link(nc.vector.tensor_tensor(total, total, none, ALU.mult))
                nc.vector.tensor_tensor(w, w, over(some), ALU.mult)
                link(nc.vector.tensor_tensor(fb, fb, over(total), ALU.mult))
                link(nc.vector.tensor_tensor(w, w, fb, ALU.add))
                link(nc.vector.tensor_reduce(wsum, w, AX.X, ALU.add))
                link(nc.vector.tensor_scalar(rtotal, wsum, TINY, None, ALU.max))
                return w, rtotal, over, link, count

            def misc_unit(g, par, n):
                kind, i, _ = MISC[n]
                if kind == "x":
                    dve.wait_ge(xh_ready, g * KC + i + 1)
                    nc.vector.tensor_tensor(xT[par][1][:, i, :], misc[(par * len(MISC) + n) % 2][:, :], xT[par][0][:, i, :],
                                            ALU.subtract).then_inc(misc_dve, 1)
                elif kind == "route":
                    w, rtotal, over, link, count = route(g, par, n)
                    link(nc.vector.reciprocal(rs[:, 0, :], rtotal))
                    link(nc.vector.tensor_tensor(wts[par][:, :, :], w, over(rs[:, 0, :]), ALU.mult))
                    assert count[0] == LINKS, count
                elif kind in ("q", "k"):
                    u = (0 if kind == "q" else KC) + i
                    dve.wait_ge(misc_act, g * MISC_ACT + emptied(n))
                    dve.wait_ge(parts_ready, g * SPLITS + u + 1)
                    nc.vector.tensor_tensor(rest[u % 2][:, :], full[u % 2][:, :], part[u % 2][:, 0, :],
                                            ALU.subtract).then_inc(rest_ready, 1)
                elif kind == "v":
                    dve.wait_ge(misc_full, g * len(MISC) + n + 1)
                    bank = misc[(par * len(MISC) + n) % 2]
                    dve.wait_ge(v_stored[i], (g + 1) * DMA)
                    nc.vector.tensor_tensor(v_sb[i][:, :, :], bank[:, :].rearrange("p (t d) -> p t d", d=D),
                                            c.bv[:, :].unsqueeze(1).broadcast_to([P, 2, D]), ALU.add).then_inc(misc_dve, 1)

            def add_expert(g, par, e):
                idx = g * E + e
                dve.wait_ge(down_used, idx * 2 + 2)
                if e == 0:
                    dve.wait_ge(base_init, g + 1)
                for hf in range(2):
                    dve.wait_ge(down_full, idx * 2 + hf + 1)
                    for j in range(2):
                        t = 2 * hf + j
                        ins = nc.vector.scalar_tensor_tensor(out=base[par][:, t, :], in0=down[hf][:, j, :], scalar=wts[par][:, t, e:e + 1],
                                                             in1=base[par][:, t, :], op0=ALU.mult, op1=ALU.add)
                    ins.then_inc(down_used, 1)

            def before():
                dve.sem_inc(rest_ready, 2)
                dve.sem_inc(hid_ready, 2)
                dve.sem_inc(down_used, 2)
                norm(0, 0, True)
                for n in range(len(MISC)):
                    misc_unit(0, 0, n)

            def body(g, par, last, more):
                for e in range(E):
                    for half in range(KC):
                        dve.wait_ge(silu_done, (g * E + e) * KC + half + 1)
                        dve.wait_ge(hl_ready, (g * E + e) * KC + half + 1)
                        nc.vector.tensor_tensor(hraw[half][:, :], gated[half][:, :], up[half][:, :], ALU.mult).then_inc(hid_ready, 1)
                    if e:
                        add_expert(g, par, e - 1)
                    if not last:
                        if e == 0:
                            norm(g + 1, 1 - par, False)
                        for n in MISC_AFTER.get(e, ()):
                            misc_unit(g + 1, 1 - par, n)
                add_expert(g, par, E - 1)

            rolled(dve, before, body)


def attention_phase(nc, a, c):
    with ExitStack() as ctx:
        sb, pb, sem = tools(nc, ctx)
        RING = 2
        kr = sb("kr", [P, RING * S], BF16)
        qr = sb("qr", [P, RING * S], BF16)
        pr = sb("pr", [P, PRING, GT], F32)
        v_all = sb("v_all", [P, NT, D], F32)
        vst = [sb(f"vst{i}", [P, KB - QUAD, VC], F32) for i in range(2)]
        vtail = sb("vtail", [P, QUAD, VC], F32)
        oT = sb("oT", [P, GT], F32)
        mx = sb("mx", [P, 2, TPG, MAXU], F32)
        nm = sb("nm", [P, TPG], F32)
        nmp = sb("nmp", [P, TPG, 2], BF16)
        osum = sb("osum", [P, TPG, HD + 1], F32)
        rden = sb("rden", [P, TPG], F32)
        sc = [pb(f"sc{i}", [P, MAXW], F32) for i in range(2)]
        st = [pb(f"st{i}", [P, GT], F32) for i in range(2)]
        pv = pb("pv", [P, GT], F32)
        post = pb("post", [P, GT], F32)

        loaded = sem("loaded")
        v_loaded = sem("v_loaded")
        v_cols = sem("v_columns_set")
        ones_set = sem("ones_set")
        sc_full = sem("sc_full")
        sc_read = sem("sc_read")
        mt_full = sem("mt_full")
        m_rows = sem("m_rows")
        st_full = sem("st_full")
        exp_done = sem("exp_done")
        pv_done = sem("pv_done")
        pv_read = sem("pv_read")
        o_full = sem("o_full")
        o_read = sem("o_read")
        v_ready = sem("v_ready")
        vt_ready = sem("vt_ready")
        passed = sem("passed_a")
        max_chain = sem("max_chain")
        out_chain = sem("out_chain")
        LOADS = 2 * len(PAIRS)
        LEAD = 2
        OUT_AT = 5

        block = ctx.enter_context(nc.Block())

        def rolled(engine, slot):
            def pairs(stage, first, end, par):
                with engine.Fori(first, end) as i:
                    for odd in range(2):
                        slot(stage, 2 * i + odd, odd, par, True, True, True)

            slot(0, 0, 0, 0, False, True, True)
            slot(0, 1, 1, 0, True, True, True)
            pairs(0, 1, QB // 2, 0)
            with engine.Fori(0, HEADS // 2 - 1) as i:
                pairs(2 * i + 1, 0, QB // 2, 1)
                pairs(2 * i + 2, 0, QB // 2, 0)
            pairs(HEADS - 1, 0, QB // 2 - 1, 1)
            slot(HEADS - 1, QB - 2, 0, 1, True, True, False)
            slot(HEADS - 1, QB - 1, 1, 1, True, False, False)

        def score_bank(kb, maxima):
            return st[kb % 2][:, :] if maxima or kb % 4 < 2 else sc[kb % 2][:, 0:GT]

        def ring(stage):
            return (stage % RING) * S

        @block.sync
        def _(sp):
            def load(n):
                h, tok = n % H, (n // H) * S
                for w, dst in ((0, qr), (1, kr)):
                    for i, pair in enumerate(PAIRS):
                        sp.dma_start(dst[i * HD:(i + 1) * HD, bass.ds(ring(n), S)],
                                     c.parts_d[w, pair[w], bass.ds(h * HD, HD), bass.ds(tok, S)]).then_inc(loaded, DMA)

            load(0)
            sp.dma_start(v_all[:, :, :], c.v_d.rearrange("(t p) d -> p t d", p=P)).then_inc(v_loaded, DMA)
            sp.wait_ge(loaded, LOADS * DMA)
            load(1)
            with sp.Fori(RING, HEADS) as n:
                wait_alone(sp, loaded, n * LOADS * DMA, passed)
                wait_alone(sp, st_full, (n - RING + 1) * QB * KB, passed)
                load(n)

        @block.gpsimd
        def _(pool):
            def v_of(n, k0, k1):
                return v_all[:, bass.ds((n // H) * KB + k0, k1 - k0), bass.ds((n % H) * HD, HD)]

            def tail(n):
                nc.gpsimd.tensor_copy(vtail[:, :, 0:HD], v_of(n, KB - QUAD, KB)).then_inc(vt_ready, 1)

            def main(n, par):
                nc.gpsimd.tensor_copy(vst[par][:, :, 0:HD], v_of(n, 0, KB - QUAD)).then_inc(v_ready, 1)

            for v in (vst[0], vst[1], vtail):
                nc.gpsimd.memset(v[:, :, HD:HD + 1], 1.0).then_inc(v_cols, 1)
                nc.gpsimd.memset(v[:, :, HD + 1:VC], 0.0).then_inc(v_cols, 1)
            pool.wait_ge(v_loaded, DMA)
            main(0, 0)
            tail(0)
            main(1, 1)

            def stage(n, par):
                wait_alone(pool, pv_done, n * QB * QUADS + 2, passed)
                tail(n)
                main(n + 1, 1 - par)

            with pool.Fori(0, HEADS // 2 - 1) as i:
                stage(2 * i + 1, 1)
                stage(2 * i + 2, 0)
            pool.wait_ge(pv_done, (HEADS - 1) * QB * QUADS + 2)
            tail(HEADS - 1)

        @block.tensor
        def _(pe):
            def max_unit(n, u):
                t, k = divmod(u, MAXU)
                stage, qb = n // QB, n % QB
                pe.wait_ge(sc_read, n * UNITS + u + 1)
                for j in range(MAXW // GT):
                    last = nc.tensor.matmul(sc[u % 2][:, j * GT:(j + 1) * GT],
                                            qr[0:ROWS, bass.ds(ring(stage) + qb * GT + t * P, P)],
                                            kr[0:ROWS, bass.ds(ring(stage) + k * MAXW + j * GT, GT)], start=True, stop=True)
                last.then_inc(sc_full, 1)

            def max_rows(n):
                pe.wait_ge(max_chain, 3 * n + 3)
                for t in range(TPG):
                    last = nc.tensor.matmul(post[ROWS:ROWSM, t * P:(t + 1) * P], nmp[:, t, :], c.identb[:, :], start=True, stop=True)
                last.then_inc(mt_full, 1)

            def scores(stage, qb, kb, maxima):
                n = (stage * QB + qb) * KB + kb
                if maxima:
                    pe.wait_ge(exp_done, n + 1)
                elif qb == QB - LEAD and kb < 2:
                    pe.wait_ge(exp_done, n + 1)
                elif qb == QB - LEAD and kb < 4:
                    pe.wait_ge(sc_read, HEADS * QB * UNITS + 2)
                else:
                    pe.wait_ge(exp_done, n - 1)
                nc.tensor.matmul(score_bank(kb, maxima), kr[0:ROWSM, bass.ds(ring(stage) + kb * P, P)],
                                 qr[0:ROWSM, bass.ds(ring(stage) + qb * GT, GT)], start=True, stop=True).then_inc(st_full, 1)

            def times_v(quad, v, exps):
                pe.wait_ge(exp_done, exps + 2)
                for j in range(QUAD):
                    last = nc.tensor.matmul(pv[VC * j:VC * (j + 1), :], v[:, j, :], pr[:, (quad % 2) * QUAD + j, :],
                                            start=(quad == 0), stop=(quad == QUADS - 1))
                last.then_inc(pv_done, 1)

            def out_back(s):
                pe.wait_ge(pv_read, s + 1)
                for t in range(TPG):
                    last = nc.tensor.transpose(post[:, t * P:(t + 1) * P], oT[:, t * P:(t + 1) * P], c.ident[:, :])
                last.then_inc(o_full, 1)

            pe.sem_inc(pv_done, 2)
            pe.wait_ge(v_cols, 6)
            pe.wait_ge(ones_set, 1)
            pe.wait_ge(loaded, LOADS * DMA)
            for n in range(LEAD):
                for u in range(UNITS):
                    max_unit(n, u)
            max_rows(0)

            def slot(stage, qb, odd, par, pending_out, pending_max, maxima):
                s = stage * QB + qb
                pe.wait_ge(m_rows, s + 1)
                if maxima:
                    pe.wait_ge(loaded, ((s + LEAD) // QB + 1) * LOADS * DMA)
                for quad in range(QUADS):
                    scores(stage, qb, 4 * quad, maxima)
                    scores(stage, qb, 4 * quad + 1, maxima)
                    if maxima:
                        max_unit(s + LEAD, 2 * quad)
                        max_unit(s + LEAD, 2 * quad + 1)
                    scores(stage, qb, 4 * quad + 2, maxima)
                    scores(stage, qb, 4 * quad + 3, maxima)
                    if quad == 0 and pending_out:
                        pe.wait_ge(vt_ready, (s - 1) // QB + 1)
                        times_v(QUADS - 1, vtail, s * KB)
                    if quad == 1:
                        pe.wait_ge(v_ready, stage + 1)
                        if pending_out:
                            pe.wait_ge(pv_read, s)
                    if quad:
                        times_v(quad - 1, vst[par][:, (quad - 1) * QUAD:quad * QUAD, :], s * KB + quad * QUAD)
                    if quad == 2 and pending_out:
                        out_back(s - 1)
                    if quad == 4 and pending_max:
                        if pending_out:
                            pe.wait_ge(o_read, s)
                        max_rows(s + 1)

            rolled(pe, slot)
            pe.wait_ge(vt_ready, HEADS)
            times_v(QUADS - 1, vtail, HEADS * QB * KB)
            pe.wait_ge(o_read, HEADS * QB - 1)
            out_back(HEADS * QB - 1)

        @block.scalar
        def _(act):
            act.sem_inc(exp_done, 2)

            def sums_read(s):
                act.wait_ge(pv_done, (s + 1) * QUADS + 2)
                nc.scalar.activation(oT[:, :], pv[:, :], ACT.Identity).then_inc(pv_read, 1)

            def rows_kept(n):
                act.wait_ge(mt_full, n + 1)
                nc.scalar.activation(qr[ROWS:ROWSM, bass.ds(ring(n // QB) + (n % QB) * GT, GT)],
                                     post[ROWS:ROWSM, :], ACT.Identity).then_inc(m_rows, 1)

            rows_kept(0)

            def slot(stage, qb, odd, par, pending_out, pending_max, maxima):
                s = stage * QB + qb
                for kb in range(KB):
                    if kb % QUAD == 0:
                        act.wait_ge(pv_done, s * QUADS + kb // QUAD + 1)
                    act.wait_ge(st_full, s * KB + kb + 1)
                    nc.scalar.activation(pr[:, kb % PRING, :], score_bank(kb, maxima), ACT.Exp).then_inc(exp_done, 1)
                    if kb == QUAD - 1 and pending_out:
                        sums_read(s - 1)
                    if kb == 6 * QUAD - 1 and pending_max:
                        rows_kept(s + 1)

            rolled(act, slot)
            sums_read(HEADS * QB - 1)

        @block.vector
        def _(dve):
            dve.sem_inc(sc_read, 2)
            dve.sem_inc(out_chain, 1)
            nc.vector.memset(kr[ROWS:ROWSM, :], 1.0).then_inc(ones_set, 1)

            def max_unit(n, u, odd):
                dve.wait_ge(sc_full, n * UNITS + u + 1)
                nc.vector.reduce_max(mx[:, odd, u // MAXU, u % MAXU:u % MAXU + 1], sc[u % 2][:, :], AX.X).then_inc(sc_read, 1)

            def negated(n, odd):
                dve.wait_ge(sc_read, (n + 1) * UNITS + 2)
                nc.vector.tensor_reduce(nm[:, :], mx[:, odd, :, :], AX.X, ALU.max, negate=True).then_inc(max_chain, 1)

            def high_part(n):
                dve.wait_ge(max_chain, 3 * n + 1)
                if not isinstance(n, int) or n:
                    dve.wait_ge(mt_full, n)
                nc.vector.tensor_copy(nmp[:, :, 0], nm[:, :]).then_inc(max_chain, 1)

            def low_part(n):
                dve.wait_ge(max_chain, 3 * n + 2)
                nc.vector.tensor_tensor(nmp[:, :, 1], nm[:, :], nmp[:, :, 0], ALU.subtract).then_inc(max_chain, 1)

            def added(s):
                dve.wait_ge(out_chain, 2 * s + 1)
                dve.wait_ge(o_full, s + 1)
                o = post[:, :].rearrange("p (t j v) -> p t v j", t=TPG, v=VC)[:, :, 0:HD + 1, :]
                nc.vector.tensor_reduce(osum[:, :, :], o, AX.X, ALU.add).then_inc(o_read, 1)

            def inverted(s):
                dve.wait_ge(o_read, s + 1)
                nc.vector.reciprocal(rden[:, :], osum[:, :, HD]).then_inc(out_chain, 1)

            def kept(s):
                stage, qb = s // QB, s % QB
                dve.wait_ge(out_chain, 2 * s + 2)
                nc.vector.tensor_tensor(c.attn[:, bass.ds((stage // H) * KB + qb * TPG, TPG), bass.ds((stage % H) * HD, HD)],
                                        osum[:, :, 0:HD], rden[:, :].unsqueeze(2).broadcast_to([P, TPG, HD]),
                                        ALU.mult).then_inc(out_chain, 1)

            for n in range(LEAD):
                for u in range(UNITS):
                    max_unit(n, u, n % 2)
                negated(n, n % 2)
                if n < LEAD - 1:
                    high_part(n)
                    low_part(n)

            def slot(stage, qb, odd, par, pending_out, pending_max, maxima):
                s = stage * QB + qb
                for u in range(UNITS):
                    if maxima:
                        max_unit(s + LEAD, u, odd)
                    if pending_max:
                        if u == 1:
                            high_part(s + 1)
                        if u == 3:
                            low_part(s + 1)
                    if pending_out:
                        if u == OUT_AT:
                            added(s - 1)
                        if u == OUT_AT + 2:
                            inverted(s - 1)
                        if u == OUT_AT + 4:
                            kept(s - 1)
                if maxima:
                    negated(s + LEAD, odd)

            rolled(dve, slot)
            for last_step in (added, inverted, kept):
                last_step(HEADS * QB - 1)


def output_phase(nc, a, c):
    with ExitStack() as ctx:
        sb, pb, sem = tools(nc, ctx)
        base = [sb(f"o_base{i}", [P, TPG, D], F32) for i in range(2)]
        att = [sb(f"att{i}", [P, TPG, D], F32) for i in range(2)]
        attT = [[sb(f"attT{i}{hl}", [P, KC, GT], F32R) for hl in range(2)] for i in range(2)]
        tp = [[pb(f"tp{i}{k}", [P, GT], F32) for k in range(KC)] for i in range(2)]
        ob = [[pb(f"ob{i}{k}", [P, 2, D], F32) for k in range(2)] for i in range(2)]
        passed = sem("passed_o")
        base_in = [sem(f"base_in{i}") for i in range(2)]
        stored = [sem(f"stored{i}") for i in range(2)]
        att_ready = sem("att_ready")
        tp_full = sem("tp_full")
        high_ready = sem("attT_high_ready")
        low_ready = sem("attT_low_ready")
        ob_full = sem("ob_full")
        sum_ready = sem("sum_ready")
        block = ctx.enter_context(nc.Block())

        def tokens_of(dram, g):
            return dram[bass.ds(g * GT, GT), :].rearrange("(t p) d -> p t d", p=P)

        def rolled(engine, body):
            with engine.Fori(0, NG // 2 - 1) as gg:
                body(2 * gg, 0, True)
                body(2 * gg + 1, 1, True)
            body(NG - 2, 0, True)
            body(NG - 1, 1, False)

        @block.sync
        def _(sp):
            def load(g, par):
                wait_alone(sp, stored[par], (g // 2 + 1) * DMA, passed)
                sp.dma_start(base[par][:, :, :], tokens_of(c.base_d, g)).then_inc(base_in[par], DMA)

            def body(g, par, more):
                if more:
                    load(g + 1, 1 - par)
                wait_alone(sp, sum_ready, g + 1 + 2, passed)
                sp.dma_start(tokens_of(a["out"], g), base[par][:, :, :]).then_inc(stored[par], DMA)

            sp.sem_inc(stored[0], DMA)
            sp.sem_inc(stored[1], DMA)
            load(0, 0)
            rolled(sp, body)
            for i in range(2):
                sp.wait_ge(stored[i], (NG // 2 + 1) * DMA)

        @block.gpsimd
        def _(pool):
            def body(g, par, more):
                wait_alone(pool, high_ready, g * KC + 2, passed)
                nc.gpsimd.tensor_copy(att[par][:, :, :], c.attn[:, bass.ds(g * TPG, TPG), :]).then_inc(att_ready, 1)

            rolled(pool, body)

        @block.tensor
        def _(pe):
            def turn(g, par):
                pe.wait_ge(att_ready, g + 1)
                for k in range(KC):
                    pe.wait_ge(low_ready, g * KC + k + 1)
                    for t in range(TPG):
                        last = nc.tensor.transpose(tp[par][k][:, t * P:(t + 1) * P], att[par][:, t, k * P:(k + 1) * P], c.ident[:, :])
                    last.then_inc(tp_full, 1)

            def body(g, par, more):
                if more:
                    turn(g + 1, 1 - par)
                pe.wait_ge(low_ready, g * KC + KC + 4)
                pe.wait_ge(sum_ready, g + 1)
                for t in range(TPG):
                    last = product(nc, ob[par][t // 2][:, t % 2, :], [[v[:, k, t * P:(t + 1) * P] for v in attT[par]] for k in range(KC)],
                                   [[v[:, k, :] for v in c.woT] for k in range(KC)])
                last.then_inc(ob_full, 1)

            turn(0, 0)
            rolled(pe, body)

        @block.scalar
        def _(act):
            def body(g, par, more):
                for k in range(KC):
                    act.wait_ge(tp_full, g * KC + k + 1)
                    if k == 0:
                        act.wait_ge(sum_ready, g + 1)
                    nc.scalar.activation(attT[par][0][:, k, :], tp[par][k][:, :], ACT.Identity).then_inc(high_ready, 1)

            act.sem_inc(high_ready, 4)
            rolled(act, body)

        @block.vector
        def _(dve):
            def low(g, par):
                dve.wait_ge(sum_ready, g + 1)
                for k in range(KC):
                    dve.wait_ge(high_ready, g * KC + k + 1 + 4)
                    nc.vector.tensor_tensor(attT[par][1][:, k, :], tp[par][k][:, :], attT[par][0][:, k, :],
                                            ALU.subtract).then_inc(low_ready, 1)

            def body(g, par, more):
                if more:
                    low(g + 1, 1 - par)
                dve.wait_ge(ob_full, g + 1)
                dve.wait_ge(base_in[par], (g // 2 + 1) * DMA)
                for i in range(2):
                    ins = nc.vector.tensor_tensor(base[par][:, 2 * i:2 * i + 2, :], ob[par][i][:, :, :], base[par][:, 2 * i:2 * i + 2, :], ALU.add)
                ins.then_inc(sum_ready, 1)

            dve.sem_inc(sum_ready, 2)
            dve.sem_inc(low_ready, 4)
            low(0, 0)
            rolled(dve, body)


class Kept:
    pass


def layer(nc, x, Wq, bq, Wk, bk, Wv, bv, Wo, bo, Wg, Wu, Wd, Wr, temperature, out):
    a = {"x": x.rearrange("b s d -> (b s) d"), "Wq": Wq, "bq": bq, "Wk": Wk, "bk": bk, "Wv": Wv, "bv": bv, "Wo": Wo, "bo": bo,
         "Wg": Wg, "Wu": Wu, "Wd": Wd, "Wr": Wr, "temperature": temperature, "out": out.rearrange("b s d -> (b s) d")}
    c = Kept()
    c.parts_d = nc.dram_tensor("parts_d", (2, 3, D, TOK), BF16, kind="Internal").ap()
    c.base_d = nc.dram_tensor("base_d", (TOK, D), F32, kind="Internal").ap()
    c.v_d = nc.dram_tensor("v_d", (TOK, D), F32, kind="Internal").ap()
    with ExitStack() as ctx:
        sb, _, _ = tools(nc, ctx)
        c.ident = sb("ident", [P, P], F32)
        c.identb = sb("identb", [P, P], BF16)
        c.woT = [sb(f"woT{hl}", [P, KC, D], F32R) for hl in range(2)]
        with ExitStack() as early_ctx:
            sb, _, _ = tools(nc, early_ctx)
            c.experts = [sb(f"experts{hl}", [P, 3, E, KC, FI], F32R) for hl in range(2)]
            c.wT = [[sb(f"wT{n}{hl}", [P, KC, D], F32R) for hl in range(2)] for n in range(3)] + [c.woT]
            c.wr = [sb(f"wr{hl}", [P, KC, E], F32R) for hl in range(2)]
            c.before = sb("before", [P, E, E], F32)
            c.bk, c.bqs = (sb(n, [P, KC], F32) for n in ("bk", "bqs"))
            c.bv, c.bo = sb("bv", [P, D], F32), sb("bo", [P, D], F32)
            c.rtemp, c.eps = (sb(n, [P, 1], F32) for n in ("rtemp", "eps"))
            setup_phase(nc, a, c)
            token_phase(nc, a, c)
        c.attn = ctx.enter_context(nc.sbuf_tensor("attn", [P, NT, D], F32))
        attention_phase(nc, a, c)
        output_phase(nc, a, c)


_INS = ["L0_attn_hidden_states", "L0_attn_Wq", "L0_attn_bq", "L0_attn_Wk", "L0_attn_bk", "L0_attn_Wv", "L0_attn_bv", "L0_attn_Wo",
        "L0_attn_bo", "L0_ffn_Wg", "L0_ffn_Wu", "L0_ffn_Wd", "L0_ffn_Wr", "L0_ffn_temperature"]


def kernel(**inputs):
    import numpy as _np
    import concourse.bacc as _bacc
    from concourse.bass_utils import run_bass_kernel_spmd as _run

    nc = _bacc.Bacc("TRN2", target_bir_lowering=False, num_devices=1)
    arrays, args = {}, []
    for name in _INS:
        arr = _np.ascontiguousarray(inputs[name])
        arrays[f"in_{name}"] = arr
        args.append(nc.dram_tensor(f"in_{name}", arr.shape, mybir.dt.from_np(arr.dtype), kind="ExternalInput").ap())
    args.append(nc.dram_tensor("out_0", (B, S, D), F32, kind="ExternalOutput").ap())
    layer(nc, *args)
    return _run(nc, [arrays], core_ids=[0]).results[0]["out_0"]
```
